# Optimizing a Trainium2 kernel written in Bass

```python
import numpy as np
import jax
import jax.numpy as jnp

def _softmax(x, axis=-1):
    return jax.nn.softmax(x, axis=axis)
def _gelu(x):
    return jax.nn.gelu(x, approximate=True)
def _silu(x):
    return jax.nn.silu(x)
def _sigmoid(x):
    return jax.nn.sigmoid(x)
def _layernorm(x, axis=-1, eps=1e-5):
    m = jnp.mean(x, axis=axis, keepdims=True)
    v = jnp.var(x, axis=axis, keepdims=True)
    return (x - m) / jnp.sqrt(v + eps)
def _scatter_add(tgt, idx, src, axis=0):
    return tgt.at[idx].add(src)
def _segment_sum(src, seg, n):
    return jax.ops.segment_sum(src, seg, n)

kernel_name = 'mk_conv_preact_d1_conv_nchw128_4cbdc0'

def setup_inputs(seed: int = 0):
    np.random.seed(seed)
    _w = jnp.asarray
    def _rec_inputs():
        import jax
        import jax.numpy as jnp
        _gk = jax.random.key(seed)
        x = -9.26e-05 + 0.9999 * jax.random.normal(jax.random.fold_in(_gk, 1), (32, 128, 96, 96), jnp.float32)
        return x
    x = _rec_inputs()
    def _L0_conv_setup():
        import jax, jax.numpy as jnp
        import numpy as np
        from jax import lax
        K = 3
        PAD = (K - 1) // 2

        def _conv1x1(x, w, b):
            return jnp.einsum('nchw,oc->nohw', x, w) + b[None, :, None, None]
        key = jax.random.key(seed)
        ks = jax.random.split(key, 8)
        N, C, H, W = (32, 128, 96, 96)
        m = 4
        Cm = C // m
        planes = 128
        x = jax.random.normal(ks[0], (N, C, H, W), jnp.float32)
        w1 = jax.random.normal(ks[1], (Cm, C), jnp.float32) * 0.05
        b1 = jax.random.normal(ks[2], (Cm,), jnp.float32) * 0.05
        wk = jax.random.normal(ks[3], (Cm,), jnp.float32) * 0.05
        bk = jax.random.normal(ks[4], (Cm,), jnp.float32) * 0.05
        b_adap = jax.random.normal(ks[5], (Cm,), jnp.float32) * 0.05
        w_fuse = jax.random.normal(ks[6], (planes, Cm), jnp.float32) * 0.05
        b_fuse = jax.random.normal(ks[7], (planes,), jnp.float32) * 0.05
        return {'x': x, 'w1': w1, 'b1': b1, 'wk': wk, 'bk': bk, 'b_adap': b_adap, 'w_fuse': w_fuse, 'b_fuse': b_fuse}
    _L0_conv_all = _L0_conv_setup()
    _L0_conv_in = {k: v for k, v in _L0_conv_all.items() if k in ('w1', 'b1', 'wk', 'bk', 'b_adap', 'w_fuse', 'b_fuse', )}
    del _L0_conv_all

    return {
        "x": x,
        "L0_conv_w1": _L0_conv_in["w1"],
        "L0_conv_b1": _L0_conv_in["b1"],
        "L0_conv_wk": _L0_conv_in["wk"],
        "L0_conv_bk": _L0_conv_in["bk"],
        "L0_conv_b_adap": _L0_conv_in["b_adap"],
        "L0_conv_w_fuse": _L0_conv_in["w_fuse"],
        "L0_conv_b_fuse": _L0_conv_in["b_fuse"],
    }

def reference(x, L0_conv_w1, L0_conv_b1, L0_conv_wk, L0_conv_bk, L0_conv_b_adap, L0_conv_w_fuse, L0_conv_b_fuse):
    import jax
    import jax.numpy as jnp
    def _L0_conv_ref(x, w1, b1, wk, bk, b_adap, w_fuse, b_fuse):
        import jax, jax.numpy as jnp
        import numpy as np
        from jax import lax
        K = 3
        PAD = (K - 1) // 2

        def _conv1x1(x, w, b):
            return jnp.einsum('nchw,oc->nohw', x, w) + b[None, :, None, None]
        N, C, H, W = x.shape
        Cm = w1.shape[0]
        f = jax.nn.relu(_conv1x1(x, w1, b1))
        pooled = x.reshape(N, C, K, H // K, K, W // K).max(axis=(3, 5))
        g = jax.nn.relu(_conv1x1(pooled, w1, b1))
        W_dyn = wk[None, None, :, None, None] * g[:, :, None, :, :] + bk[None, None, :, None, None]
        y = lax.conv_general_dilated(f.reshape(1, N * Cm, H, W), W_dyn.reshape(N * Cm, Cm, K, K), window_strides=(1, 1), padding=((PAD, PAD), (PAD, PAD)), dimension_numbers=('NCHW', 'OIHW', 'NCHW'), feature_group_count=N).reshape(N, Cm, H, W) + b_adap[None, :, None, None]
        return _conv1x1(y, w_fuse, b_fuse)

    def _gn(v, G=32, eps=1e-5):
        B_, C_, H_, W_ = v.shape
        g = v.reshape(B_, G, C_ // G, H_, W_)
        m = jnp.mean(g, axis=(2, 3, 4), keepdims=True)
        s = jnp.var(g, axis=(2, 3, 4), keepdims=True)
        return ((g - m) / jnp.sqrt(s + eps)).reshape(v.shape)

    def _ln_c(v, eps=1e-6):
        m = jnp.mean(v, axis=1, keepdims=True)
        s = jnp.var(v, axis=1, keepdims=True)
        return (v - m) / jnp.sqrt(s + eps)

    def _ln_t(v, eps=1e-5):
        m = jnp.mean(v, axis=-1, keepdims=True)
        s = jnp.var(v, axis=-1, keepdims=True)
        return (v - m) / jnp.sqrt(s + eps)

    def _to_tokens(v):
        B_, C_, H_, W_ = v.shape
        return v.reshape(B_, C_, H_ * W_).transpose(0, 2, 1)
    def _from_tokens(t, like):
        B_, C_, H_, W_ = like.shape
        return t.transpose(0, 2, 1).reshape(B_, C_, H_, W_)

    x = x + _L0_conv_ref(_gn(x), L0_conv_w1, L0_conv_b1, L0_conv_wk, L0_conv_bk, L0_conv_b_adap, L0_conv_w_fuse, L0_conv_b_fuse)
    return x


_drawn_inputs = setup_inputs


def setup_inputs(seed=0):
    import zlib

    import numpy as np

    out = dict(_drawn_inputs(seed))
    spreads = {}
    factors = {'L0_conv_b_adap': 3.937}
    for name, (base, spread) in spreads.items():
        noise = np.random.default_rng([zlib.crc32(name.encode()), seed]).standard_normal(out[name].shape)
        drawn = base * np.exp(spread * noise) if base else spread * noise
        out[name] = jnp.asarray(drawn.astype(out[name].dtype))
    for name, factor in factors.items():
        out[name] = (out[name] * factor).astype(out[name].dtype)
    return out
```

```python
import numpy as np
import concourse.bass as bass
from concourse import mybir
from contextlib import ExitStack

N, C, HGT, WID = 32, 128, 96, 96
PIX = HGT * WID
CM = 32
P = 128
GROUP = C // 32
EPS = 1e-5
TAPS = 9
CHUNKS = P // CM
CROWS = HGT // CHUNKS
CPIX = CROWS * WID
FROWS, FW = CROWS + 2, WID + 2
THIRDS = 3
TPIX = PIX // THIRDS
BLK = HGT // 3
AUNITS = [(0, 5), (5, 4), (9, 4), (13, 4), (17, 4), (21, 5)]
NA = len(AUNITS)
BROWS = 4
NB = CROWS // BROWS
BPIX = BROWS * WID
BANK = 512
CU = 2 * BANK
NC = PIX // CU
NX = 4
SETS = P // 32
HEAD, REST = 0, 1


def set_taps(c):
    return [0, 1, 2] if c == 0 else [2 * c + 1, 2 * c + 2]


SLOTS = 4
TSLOT = SLOTS - 1


def conv_kernel(nc, x_d, w1_d, vec_d, wf_d, const_d, out_d):
    f32, f32r, bf16 = mybir.dt.float32, mybir.dt.float32r, mybir.dt.bfloat16
    ALU, ACT, AX = mybir.AluOpType, mybir.ActivationFunctionType, mybir.AxisListType

    ctx = ExitStack()
    with ctx:
        def sb(name, shape, dt=f32):
            return ctx.enter_context(nc.sbuf_tensor(name, shape, dt))

        def sem(name):
            return ctx.enter_context(nc.semaphore(name))

        x_sb = sb("x_sb", [P, NX, PIX])
        f_sb = sb("f_sb", [P, FROWS, FW])
        fields = [sb(f"fields{i}", [P, CPIX], f32r) for i in range(2)]
        heads = [sb(f"heads{i}", [P, BPIX], f32r) for i in range(2)]
        squares = sb("squares", [P, TPIX], bf16)
        pairs = sb("pairs", [P, TPIX // 2])
        tapw = [[sb(f"tapw{i}{h}", [P, CHUNKS * P], f32r) for h in range(2)] for i in range(2)]
        w1_sb = sb("w1_sb", [P, P])
        w1_fold = sb("w1_fold", [P, 2, P])
        wf_sb = sb("wf_sb", [P, CHUNKS, P])
        tapsel = sb("tapsel", [P, P])
        const_sb = sb("const_sb", [P, 2 * P + 6])
        group_avg = const_sb[:, 0:P]
        slotmask = const_sb[:, P:2 * P]
        restmask = const_sb[:, 2 * P:2 * P + 1]
        minus_half = const_sb[:, 2 * P + 1:2 * P + 2]
        badap_mask = const_sb[:, 2 * P + 2:2 * P + 3]
        one_half_more = const_sb[:, 2 * P + 3:2 * P + 4]
        per_pixel = const_sb[:, 2 * P + 4:2 * P + 6]
        zeros = sb("zeros", [P, WID])
        vec_sb = sb("vec_sb", [P, 5])
        b1, wk, bk, badap, bfuse = (vec_sb[:, i:i + 1] for i in range(5))
        tapcols = sb("tapcols", [P, 3, 32])
        zbias = sb("zbias", [P, 1])
        badap0 = sb("badap0", [P, 1])
        stats = sb("stats", [P, 2, THIRDS, 2])
        pooled = sb("pooled", [P, 2, TAPS + 1])
        fbias = sb("fbias", [P, 2])
        gates = sb("gates", [P, 2, TAPS])
        sm = sb("sm", [P, 24])
        var_eps = sb("var_eps", [P, 1])

        ab_ps = [ctx.enter_context(nc.psum_tensor(f"ab_ps{i}", [P, BANK], f32)) for i in range(3)]
        c_ps = [ctx.enter_context(nc.psum_tensor(f"c_ps{i}", [P, 2, BANK], f32)) for i in range(2)]
        small_ps = ctx.enter_context(nc.psum_tensor("small_ps", [P, BANK], f32))
        mean_ps, var_ps = small_ps[:, 0:1], small_ps[:, 1:2]
        gate_ps = small_ps[:, 2:2 + TAPS + 1]
        zb_ps = small_ps[:, 16:17]

        w_loaded = sem("w_loaded")
        wf_zeroed = sem("wf_zeroed")
        wf_loaded = sem("wf_loaded")
        tapcols_zeroed = sem("tapcols_zeroed")
        ready_dve = sem("ready_dve")
        ready_pool = sem("ready_pool")
        zb_summed = sem("zb_summed")
        x_loaded = [[sem(f"x_loaded{b}{t}") for t in range(THIRDS)] for b in range(NX)]
        x_stored = [[sem(f"x_stored{b}{t}") for t in range(THIRDS)] for b in range(NX)]
        pairs_ready = sem("pairs_ready")
        squared = sem("squared")
        summed = sem("summed")
        maxed = sem("maxed")
        pool_step = sem("pool_step")
        mean_own = sem("mean_own")
        mean_summed = sem("mean_summed")
        mean_ready = sem("mean_ready")
        spread_own = sem("spread_own")
        var_summed = sem("var_summed")
        var_ready = sem("var_ready")
        fold_ready = sem("fold_ready")
        gates_summed = sem("gates_summed")
        fbias_ready = sem("fbias_ready")
        gates_ready = sem("gates_ready")
        tapsel_ready = sem("tapsel_ready")
        tapw_summed = sem("tapw_summed")
        tapw_head = sem("tapw_head")
        tapw_rest = sem("tapw_rest")
        ab_summed = sem("ab_summed")
        f_ready = sem("f_ready")
        edges_zeroed = sem("edges_zeroed")
        head_ready = sem("head_ready")
        fields_ready = sem("fields_ready")
        c_summed = sem("c_summed")
        c_added = sem("c_added")

        class Img:

            def __init__(self, it, k):
                self.it, self.k = it, k
                self.buf, self.par = k % NX, k % 2

            def __add__(self, d):
                return Img(self.it, self.k + d)

            def n(self, per, more):
                if isinstance(self.it, int):
                    return (NX * self.it + self.k) * per + more
                assert self.k * per + more > 0
                return self.it * (NX * per) + (self.k * per + more)

            def use(self, more):
                if isinstance(self.it, int):
                    return 16 * (self.it + self.k // NX + more)
                assert self.k // NX + more > 0
                return self.it * 16 + 16 * (self.k // NX + more)

            def dram(self, ap, t):
                if isinstance(self.it, int):
                    return ap[NX * self.it + self.k, :, t * TPIX:(t + 1) * TPIX]
                return ap[bass.ds(self.it * NX + self.k, 1), :, t * TPIX:(t + 1) * TPIX].rearrange(
                    "o c w -> (o c) w")

        def wait(eng, s, value):
            if not isinstance(value, int) or value > 0:
                eng.wait_ge(s, value)

        def xt(img, t):
            return x_sb[:, img.buf, t * TPIX:(t + 1) * TPIX]

        def run_slots(eng, slot, first=2):
            trips = (N - 4) // NX
            for s in range(-2, first):
                slot(Img(0, s), s)
            with eng.Fori(0, trips) as it:
                for j in range(first, first + NX):
                    slot(Img(it, j), None)
            for s in range(first + trips * NX, N + 1):
                slot(Img(0, s), s)

        def has(s, d):
            return s is None or 0 <= s + d < N

        block = ctx.enter_context(nc.Block())

        @block.sync
        def _(sp):
            sp.dma_start(const_sb[:], const_d).then_inc(w_loaded, 16)
            sp.dma_start(vec_sb[:], vec_d).then_inc(w_loaded, 16)
            sp.dma_start(w1_sb[:], w1_d).then_inc(w_loaded, 16)

            def load(img, t):
                wait(sp, x_stored[img.buf][t], img.use(0))
                sp.dma_start(xt(img, t), img.dram(x_d, t)).then_inc(x_loaded[img.buf][t], 16)

            for n in range(2):
                for t in range(THIRDS):
                    load(Img(0, n), t)
                    if n == 0 and t == 0:
                        sp.wait_ge(wf_zeroed, 1)
                        for q in range(CHUNKS):
                            sp.dma_start(wf_sb[q * CM:(q + 1) * CM, q, :], wf_d).then_inc(wf_loaded, 16)

            def slot(img, s):
                for t in range(THIRDS):
                    if has(s, -1):
                        old = img + -1
                        wait(sp, c_added, old.n(NC, NC // THIRDS * (t + 1)))
                        sp.dma_start(old.dram(out_d, t), xt(old, t)).then_inc(x_stored[old.buf][t], 16)
                        if t > 0 and has(s, 3):
                            load(img + 3, t - 1)
                    if has(s, 3) and (s is not None and s <= 0 and s + 3 >= 2):
                        load(img + 3, t)
                if has(s, -1) and has(s, 3) and not (s is not None and s <= 0):
                    load(img + 3, THIRDS - 1)

            run_slots(sp, slot, first=1)
            for img in range(N - NX, N):
                for t in range(THIRDS):
                    sp.wait_ge(x_stored[img % NX][t], 16 * (img // NX + 1))

        @block.gpsimd
        def _(pool):
            nc.gpsimd.memset(f_sb[:], 0.0).then_inc(ready_pool, 1)
            nc.gpsimd.memset(zeros[:], 0.0).then_inc(ready_pool, 1)
            pool.wait_ge(w_loaded, 48)
            pool.wait_ge(ready_pool, 2)
            nc.gpsimd.tensor_copy(tapsel[:], slotmask).then_inc(ready_pool, 1)
            nc.gpsimd.tensor_tensor(badap0[:], badap, badap_mask, ALU.mult).then_inc(ready_pool, 1)
            pool.wait_ge(ready_pool, 4)

            def pair(img, t):
                third = xt(img, t)
                wait(pool, x_loaded[img.buf][t], img.use(1))
                wait(pool, summed, img.n(THIRDS, t))
                nc.gpsimd.tensor_tensor(pairs[:], third[:, 0:TPIX // 2], third[:, TPIX // 2:TPIX],
                                        ALU.add).then_inc(pairs_ready, 1)

            STEPS = 13

            def fold(img):
                st = stats[:, img.par]
                done = [0]

                def then(ins):
                    ins.then_inc(pool_step, 1)
                    done[0] += 1
                    pool.wait_ge(pool_step, img.n(STEPS, done[0]))

                wait(pool, squared, img.n(THIRDS, THIRDS))
                wait(pool, summed, img.n(THIRDS, THIRDS))
                then(nc.gpsimd.tensor_tensor(sm[:, 0:2], st[:, 0, :], st[:, 1, :], ALU.add))
                then(nc.gpsimd.tensor_tensor(sm[:, 2:4], sm[:, 0:2], st[:, 2, :], ALU.add))
                nc.gpsimd.tensor_tensor(sm[:, 4:6], sm[:, 2:4], per_pixel, ALU.mult).then_inc(mean_own, 1)
                pool.wait_ge(mean_own, img.n(1, 1))
                then(nc.gpsimd.tensor_tensor(sm[:, 6:7], sm[:, 4:5], x_sb[:, img.buf, 0:1], ALU.subtract))
                then(nc.gpsimd.tensor_tensor(sm[:, 7:8], sm[:, 6:7], sm[:, 6:7], ALU.mult))
                then(nc.gpsimd.tensor_tensor(sm[:, 8:9], sm[:, 5:6], sm[:, 7:8], ALU.subtract))
                pool.wait_ge(mean_ready, img.n(1, 1))
                then(nc.gpsimd.tensor_tensor(sm[:, 9:10], sm[:, 4:5], pooled[:, img.par, TAPS:TAPS + 1],
                                             ALU.subtract))
                then(nc.gpsimd.tensor_tensor(sm[:, 10:11], sm[:, 9:10], sm[:, 9:10], ALU.mult))
                nc.gpsimd.tensor_tensor(sm[:, 11:12], sm[:, 8:9], sm[:, 10:11], ALU.add
                                        ).then_inc(spread_own, 1)
                pool.wait_ge(var_ready, img.n(1, 1))
                v, r0, rstd = var_eps[:], sm[:, 12:13], sm[:, 16:17]
                then(nc.gpsimd.tensor_tensor(r0, v, minus_half, ALU.pow))
                then(nc.gpsimd.tensor_tensor(sm[:, 17:18], v, minus_half, ALU.mult))
                then(nc.gpsimd.tensor_tensor(sm[:, 13:14], r0, r0, ALU.mult))
                then(nc.gpsimd.tensor_tensor(sm[:, 14:15], sm[:, 13:14], sm[:, 17:18], ALU.mult))
                then(nc.gpsimd.tensor_tensor(sm[:, 15:16], sm[:, 14:15], one_half_more, ALU.add))
                then(nc.gpsimd.tensor_tensor(rstd, r0, sm[:, 15:16], ALU.mult))
                wait(pool, ab_summed, (img + -2).n(NA + NB, NA))
                nc.gpsimd.tensor_tensor(w1_fold[:, img.par, :], w1_sb[:], rstd.to_broadcast([P, P]),
                                        ALU.mult).then_inc(fold_ready, 1)

            def place_gates(img):
                wait(pool, gates_ready, img.n(1, 1))
                wait(pool, tapw_summed, img.n(1, 0))
                g = gates[:, img.par, :]
                sel = tapsel[:, :].rearrange("p (c j r) -> p c j r", c=SETS, j=SLOTS)
                msk = slotmask.rearrange("p (c j r) -> p c j r", c=SETS, j=SLOTS)
                rows = 2 * CHUNKS
                nc.gpsimd.tensor_tensor(sel[:, 0, 0:3, :], msk[:, 0, 0:3, :],
                                        g[:, 0:3].rearrange("p (j r) -> p j r", r=1).to_broadcast([P, 3, rows]),
                                        ALU.mult).then_inc(tapsel_ready, 1)
                nc.gpsimd.tensor_tensor(sel[:, 1:4, 0:2, :], msk[:, 1:4, 0:2, :],
                                        g[:, 3:9].rearrange("p (c j r) -> p c j r", j=2, r=1
                                                            ).to_broadcast([P, 3, 2, rows]),
                                        ALU.mult).then_inc(tapsel_ready, 1)

            def zero_edge(img, first, has_pairs=True):
                if first:
                    wait(pool, tapsel_ready, img.n(2, 2))
                elif has_pairs:
                    wait(pool, pairs_ready, (img + 2).n(THIRDS, 1))
                wait(pool, f_ready, img.n(NA, 1 if first else NA))
                edge = f_sb[0:CM, 0, 1:1 + WID] if first else f_sb[P - CM:P, FROWS - 1, 1:1 + WID]
                z = zeros[0:CM, :] if first else zeros[P - CM:P, :]
                nc.gpsimd.tensor_tensor(edge, z, z, ALU.add).then_inc(edges_zeroed, 1)

            def slot(img, s):
                if has(s, 1):
                    fold(img + 1)
                if has(s, 0):
                    place_gates(img)
                    zero_edge(img, True)
                    pool.wait_ge(edges_zeroed, img.n(2, 1))
                if has(s, 2):
                    pair(img + 2, 0)
                if has(s, 0):
                    zero_edge(img, False, has(s, 2))
                    pool.wait_ge(edges_zeroed, img.n(2, 2))
                if has(s, 2):
                    pair(img + 2, 1)
                    pair(img + 2, 2)

            run_slots(pool, slot)

        @block.scalar
        def _(act):
            act.wait_ge(ready_dve, 1)
            act.wait_ge(ready_pool, 1)

            def square(img, t):
                wait(act, x_loaded[img.buf][t], img.use(1))
                wait(act, squared, img.n(THIRDS, t))
                nc.scalar.activation(squares[:], xt(img, t), ACT.Square, bias=x_sb[:, img.buf, 0:1],
                                     scale=-1.0, accum_out=stats[:, img.par, t, 1:2]).then_inc(squared, 1)

            def total(img, t):
                act.wait_ge(pairs_ready, img.n(THIRDS, t + 1))
                nc.scalar.activation(pairs[:], pairs[:], ACT.Copy,
                                     accum_out=stats[:, img.par, t, 0:1]).then_inc(summed, 1)

            def take_f(img, u):
                r, n = AUNITS[u]
                if u == 0:
                    act.wait_ge(fbias_ready, img.n(1, 1))
                act.wait_ge(ab_summed, img.n(NA + NB, u + 1))
                nc.scalar.activation(f_sb[:, r:r + n, 1:1 + WID],
                                     ab_ps[u % 3][:, 0:n * WID].rearrange("p (r w) -> p r w", w=WID),
                                     ACT.Relu, bias=fbias[:, img.par:img.par + 1]).then_inc(f_ready, 1)

            def head(img, u):
                act.wait_ge(ab_summed, img.n(NA + NB, NA + u + 1))
                wait(act, fields_ready, img.n(NB, u - 1))
                nc.scalar.activation(heads[u % 2][:], ab_ps[(NA + u) % 3][:, 0:BPIX],
                                     ACT.Copy).then_inc(head_ready, 1)

            def tap_head(img):
                act.wait_ge(tapw_summed, img.n(1, 1))
                nc.scalar.activation(tapw[img.par][HEAD][:], small_ps[:], ACT.Copy).then_inc(tapw_head, 1)

            def slot(img, s):
                later = img + 2
                if has(s, 2):
                    square(later, 0)
                if has(s, 0):
                    take_f(img, 0)
                    take_f(img, 1)
                    take_f(img, 2)
                if has(s, 2):
                    total(later, 0)
                if has(s, 0):
                    take_f(img, 3)
                if has(s, 2):
                    square(later, 1)
                if has(s, 0):
                    take_f(img, 4)
                    take_f(img, 5)
                if has(s, 2):
                    total(later, 1)
                if has(s, 0):
                    head(img, 0)
                    tap_head(img)
                    head(img, 1)
                if has(s, 2):
                    square(later, 2)
                if has(s, 0):
                    head(img, 2)
                    head(img, 3)
                if has(s, 2):
                    total(later, 2)
                if has(s, 0):
                    head(img, 4)
                    head(img, 5)

            run_slots(act, slot)

        @block.vector
        def _(dve):
            nc.vector.memset(wf_sb[:], 0.0).then_inc(wf_zeroed, 1)
            nc.vector.memset(tapcols[:], 0.0).then_inc(tapcols_zeroed, 1)
            for bank in ab_ps:
                last = nc.vector.memset(bank[:], 0.0)
            last.then_inc(ready_dve, 1)
            dve.wait_ge(w_loaded, 48)
            dve.wait_ge(tapcols_zeroed, 1)
            cols = tapcols[:, :, :].rearrange("p j (l q h) -> p j l q h", l=SLOTS, q=CHUNKS)
            for j in range(3):
                for q in range(CHUNKS):
                    rows = slice(q * CM, (q + 1) * CM)
                    nc.vector.tensor_copy(cols[rows, j, j, q, :], vec_sb[rows, 1:2].to_broadcast([CM, 2]))
                    last = nc.vector.tensor_copy(cols[rows, j, TSLOT, q, :],
                                                 vec_sb[rows, 2:3].to_broadcast([CM, 2]))
            last.then_inc(ready_dve, 1)
            dve.wait_ge(zb_summed, 1)
            nc.vector.tensor_tensor(zbias[:], zb_ps, bfuse, ALU.add).then_inc(ready_dve, 1)
            dve.wait_ge(ready_dve, 3)

            def block_max(img, t):
                wait(dve, x_loaded[img.buf][t], img.use(1))
                wait(dve, gates_summed, img.n(1, -1))
                nc.vector.tensor_reduce(pooled[:, img.par, 3 * t:3 * t + 3],
                                        xt(img, t).rearrange("p (h a w) -> p a h w", h=BLK, a=3),
                                        AX.XY, ALU.max).then_inc(maxed, 1)

            def take_mean(img):
                dve.wait_ge(mean_summed, img.n(1, 1))
                nc.vector.tensor_copy(pooled[:, img.par, TAPS:TAPS + 1], mean_ps).then_inc(mean_ready, 1)

            def take_var(img):
                dve.wait_ge(var_summed, img.n(1, 1))
                nc.vector.tensor_scalar(var_eps[:], var_ps, EPS, None, ALU.add).then_inc(var_ready, 1)

            def take_gates(img):
                bias = fbias[:, img.par:img.par + 1]
                dve.wait_ge(gates_summed, img.n(1, 1))
                nc.vector.scalar_tensor_tensor(bias, gate_ps[:, TAPS:TAPS + 1], -1.0, b1, ALU.mult,
                                               ALU.add).then_inc(fbias_ready, 1)
                dve.wait_ge(fbias_ready, img.n(1, 1))
                wait(dve, tapsel_ready, (img + -2).n(2, 2))
                nc.vector.tensor_scalar(gates[:, img.par, :], gate_ps[:, 0:TAPS], bias, 0.0, ALU.add,
                                        ALU.max).then_inc(gates_ready, 1)

            def tap_rest(img):
                dve.wait_ge(tapw_head, img.n(1, 1))
                nc.vector.tensor_tensor(tapw[img.par][REST][:], small_ps[:], tapw[img.par][HEAD][:],
                                        ALU.subtract).then_inc(tapw_rest, 1)

            def split(img, u):
                dve.wait_ge(head_ready, img.n(NB, u + 1))
                nc.vector.scalar_tensor_tensor(fields[img.par][:, u * BPIX:(u + 1) * BPIX], heads[u % 2][:],
                                               restmask, ab_ps[(NA + u) % 3][:, 0:BPIX], ALU.mult,
                                               ALU.add).then_inc(fields_ready, 1)

            def add(img, u):
                dve.wait_ge(c_summed, img.n(NC, u + 1))
                part = x_sb[:, img.buf, u * CU:(u + 1) * CU].rearrange("p (b w) -> p b w", b=2)
                nc.vector.scalar_tensor_tensor(part, c_ps[(img.k + u) % 2][:], zbias[:], part, ALU.add,
                                               ALU.add).then_inc(c_added, 1)

            def slot(img, s):
                done, later = img + -1, img + 2

                def adds(us):
                    if has(s, -1):
                        for u in us:
                            add(done, u)

                def splits(u):
                    if has(s, 0):
                        split(img, u)

                if has(s, 2):
                    block_max(later, 0)
                adds([0])
                if has(s, 1):
                    take_mean(img + 1)
                adds([1, 2])
                if has(s, 1):
                    take_var(img + 1)
                adds([3])
                if has(s, 2):
                    block_max(later, 1)
                splits(0)
                if has(s, 1):
                    take_gates(img + 1)
                adds([4])
                if has(s, 0):
                    tap_rest(img)
                splits(1)
                adds([5])
                splits(2)
                adds([6])
                if has(s, 2):
                    block_max(later, 2)
                splits(3)
                adds([7])
                splits(4)
                adds([8])
                splits(5)

            run_slots(dve, slot)

        @block.tensor
        def _(pe):
            pe.wait_ge(wf_loaded, 16 * CHUNKS)
            pe.wait_ge(ready_pool, 4)
            nc.tensor.matmul(zb_ps, wf_sb[:, 0, :], badap0[:], start=True, stop=True).then_inc(zb_summed, 1)
            pe.wait_ge(ready_dve, 3)

            def unit_free(img, u):
                if u >= 3 and u - 3 < NA:
                    pe.wait_ge(f_ready, img.n(NA, u - 2))
                elif u >= 3:
                    pe.wait_ge(fields_ready, img.n(NB, u - 2 - NA))
                else:
                    wait(pe, fields_ready, img.n(NB, u - 2))

            def conv_a(img, u):
                r, n = AUNITS[u]
                if u == 0:
                    pe.wait_ge(fold_ready, img.n(1, 1))
                unit_free(img, u)
                for q in range(CHUNKS):
                    lo, hi = max(CROWS * q + r - 1, 0), min(CROWS * q + r - 1 + n, HGT)
                    at = (lo - (CROWS * q + r - 1)) * WID
                    last = nc.tensor.matmul(ab_ps[u % 3][q * CM:(q + 1) * CM, at:at + (hi - lo) * WID],
                                            w1_fold[:, img.par, 0:CM], x_sb[:, img.buf, lo * WID:hi * WID],
                                            start=True, stop=True)
                last.then_inc(ab_summed, 1)

            def taps_b(img, u):
                unit_free(img, NA + u)
                pe.wait_ge(f_ready, img.n(NA, min(u + 2, NA)))
                if u == 0:
                    pe.wait_ge(edges_zeroed, img.n(2, 1))
                if u == NB - 1:
                    pe.wait_ge(edges_zeroed, img.n(2, 2))
                for j in range(3):
                    for c in range(SETS):
                        taps = set_taps(c)
                        if j < len(taps):
                            kh, kw = taps[j] // 3, taps[j] % 3
                            last = nc.tensor.matmul(
                                ab_ps[(NA + u) % 3][32 * c:32 * c + 32, 0:BPIX], tapcols[:, j, :],
                                f_sb[:, BROWS * u + kh:BROWS * (u + 1) + kh, kw:kw + WID],
                                start=(j == 0), stop=(j == len(taps) - 1))
                last.then_inc(ab_summed, 1)

            def conv_c(img, u):
                if u == 0:
                    pe.wait_ge(fields_ready, img.n(NB, NB))
                    pe.wait_ge(tapw_rest, img.n(1, 1))
                wait(pe, c_added, img.n(NC, u - 1))
                for h in range(2):
                    a = u * CU + h * BANK
                    while a < u * CU + (h + 1) * BANK:
                        q = a // CPIX
                        b = min((q + 1) * CPIX, u * CU + (h + 1) * BANK)
                        o = a - u * CU - h * BANK
                        for part in (HEAD, REST):
                            last = nc.tensor.matmul(c_ps[(img.k + u) % 2][:, h, o:o + b - a],
                                                    tapw[img.par][part][:, q * P:(q + 1) * P],
                                                    fields[img.par][:, a - q * CPIX:b - q * CPIX],
                                                    start=(part == HEAD), stop=(part == REST))
                        a = b
                last.then_inc(c_summed, 1)

            def sum_mean(img):
                pe.wait_ge(mean_own, img.n(1, 1))
                wait(pe, gates_ready, img.n(1, 0))
                wait(pe, tapw_rest, img.n(1, -1))
                nc.tensor.matmul(mean_ps, group_avg, sm[:, 4:5], start=True, stop=True
                                 ).then_inc(mean_summed, 1)

            def sum_var(img):
                pe.wait_ge(spread_own, img.n(1, 1))
                nc.tensor.matmul(var_ps, group_avg, sm[:, 11:12], start=True, stop=True
                                 ).then_inc(var_summed, 1)

            def sum_gates(img):
                pe.wait_ge(fold_ready, img.n(1, 1))
                pe.wait_ge(maxed, img.n(THIRDS, THIRDS))
                nc.tensor.matmul(gate_ps, w1_fold[:, img.par, :], pooled[:, img.par, :], start=True,
                                 stop=True).then_inc(gates_summed, 1)

            def sum_tapw(img, s):
                pe.wait_ge(tapsel_ready, img.n(2, 2))
                if has(s, 1):
                    pe.wait_ge(gates_ready, img.n(1, 2))
                nc.tensor.matmul(small_ps[:], tapsel[:], wf_sb[:, :, :].rearrange("p q o -> p (q o)"),
                                 start=True, stop=True).then_inc(tapw_summed, 1)

            def slot(img, s):
                done = img + -1

                def a(u):
                    if has(s, 0):
                        conv_a(img, u)

                def b(u):
                    if has(s, 0):
                        taps_b(img, u)

                def c(u):
                    if has(s, -1):
                        conv_c(done, u)

                a(0)
                a(1)
                c(0)
                if has(s, 1):
                    sum_mean(img + 1)
                a(2)
                c(1)
                a(3)
                c(2)
                if has(s, 1):
                    sum_var(img + 1)
                a(4)
                c(3)
                a(5)
                b(0)
                if has(s, 1):
                    sum_gates(img + 1)
                c(4)
                b(1)
                if has(s, 0):
                    sum_tapw(img, s)
                c(5)
                b(2)
                c(6)
                b(3)
                c(7)
                b(4)
                c(8)
                b(5)

            run_slots(pe, slot)


def constants():
    k = np.arange(P)
    out = np.zeros((P, 2 * P + 6), np.float32)
    out[:, 0:P] = (k[:, None] // GROUP == k[None, :] // GROUP) / GROUP
    for c in range(SETS):
        for j in [*range(len(set_taps(c))), TSLOT]:
            for q in range(CHUNKS):
                at = P + 32 * c + 8 * j + 2 * q
                out[q * CM:(q + 1) * CM, at:at + 2] = 1.0
    out[:, 2 * P] = -(k % 2)
    out[:, 2 * P + 1] = -0.5
    out[:, 2 * P + 2] = k < CM
    out[:, 2 * P + 3] = 1.5
    out[:, 2 * P + 4:] = 1.0 / PIX
    return out


def kernel(x, L0_conv_w1, L0_conv_b1, L0_conv_wk, L0_conv_bk, L0_conv_b_adap, L0_conv_w_fuse,
           L0_conv_b_fuse):
    import concourse.bacc as _bacc
    from concourse.bass_utils import run_bass_kernel_spmd as _run

    rep = [np.tile(np.asarray(v), CHUNKS) for v in (L0_conv_b1, L0_conv_wk, L0_conv_bk, L0_conv_b_adap)]
    arrays = {
        "x_in": np.ascontiguousarray(x).reshape(N, C, PIX),
        "w1_in": np.ascontiguousarray(np.tile(np.asarray(L0_conv_w1).T, (1, CHUNKS))),
        "vec_in": np.ascontiguousarray(np.stack([*rep, np.asarray(L0_conv_b_fuse)], axis=1)),
        "wf_in": np.ascontiguousarray(np.asarray(L0_conv_w_fuse).T),
        "const_in": constants(),
    }
    nc = _bacc.Bacc("TRN2", target_bir_lowering=False, num_devices=1)
    aps = [nc.dram_tensor(n, a.shape, mybir.dt.from_np(a.dtype), kind="ExternalInput").ap()
           for n, a in arrays.items()]
    out = nc.dram_tensor("x_out", (N, C, PIX), mybir.dt.float32, kind="ExternalOutput").ap()
    conv_kernel(nc, *aps, out)
    r = _run(nc, [arrays], core_ids=[0])
    return r.results[0]["x_out"].reshape(N, C, HGT, WID)
```

```python
import numpy as np
import concourse.bass as bass
from concourse import mybir
from contextlib import ExitStack

N, C, HGT, WID = 32, 128, 96, 96
PIX = HGT * WID
CM = 32
P = 128
GROUP = C // 32
EPS = 1e-5
TAPS = 9
CHUNKS = P // CM
CROWS = HGT // CHUNKS
CPIX = CROWS * WID
FROWS, FW = CROWS + 2, WID + 2
THIRDS = 3
TPIX = PIX // THIRDS
BLK = HGT // 3
AUNITS = [(0, 5), (5, 4), (9, 4), (13, 4), (17, 4), (21, 5)]
NA = len(AUNITS)
BROWS = 4
NB = CROWS // BROWS
BPIX = BROWS * WID
BANK = 512
CU = 2 * BANK
NC = PIX // CU
NX = 4
SETS = P // 32
HEAD, REST = 0, 1


SLOTS = 4
LAST, TSLOT = 2, 3
POOL_ADDS = (4, 7)


def dve_adds(u):
    return u - sum(v < u for v in POOL_ADDS)


def conv_kernel(nc, x_d, w1_d, vec_d, wf_d, const_d, out_d):
    f32, f32r, bf16 = mybir.dt.float32, mybir.dt.float32r, mybir.dt.bfloat16
    ALU, ACT, AX = mybir.AluOpType, mybir.ActivationFunctionType, mybir.AxisListType

    ctx = ExitStack()
    with ctx:
        def sb(name, shape, dt=f32):
            return ctx.enter_context(nc.sbuf_tensor(name, shape, dt))

        def sem(name):
            return ctx.enter_context(nc.semaphore(name))

        x_sb = sb("x_sb", [P, NX, PIX])
        f_sb = sb("f_sb", [P, FROWS, FW])
        fields = [sb(f"fields{i}", [P, CPIX], f32r) for i in range(2)]
        heads = [sb(f"heads{i}", [P, BPIX], f32r) for i in range(2)]
        z_sb = sb("z_sb", [P, 2, BANK])
        squares = sb("squares", [P, TPIX // 2], bf16)
        pairs = sb("pairs", [P, TPIX // 2])
        tapw = [[sb(f"tapw{i}{h}", [P, CHUNKS * P], f32r) for h in range(2)] for i in range(2)]
        w1_sb = sb("w1_sb", [P, P])
        w1_fold = sb("w1_fold", [P, 2, P])
        wf_sb = sb("wf_sb", [P, CHUNKS, P])
        tapsel = sb("tapsel", [P, P])
        const_sb = sb("const_sb", [P, 2 * P + 6])
        group_avg = const_sb[:, 0:P]
        slotmask = const_sb[:, P:2 * P]
        restmask = const_sb[:, 2 * P:2 * P + 1]
        minus_half = const_sb[:, 2 * P + 1:2 * P + 2]
        badap_mask = const_sb[:, 2 * P + 2:2 * P + 3]
        one_half_more = const_sb[:, 2 * P + 3:2 * P + 4]
        per_pixel = const_sb[:, 2 * P + 4:2 * P + 5]
        vec_sb = sb("vec_sb", [P, 5])
        b1, wk, bk, badap, bfuse = (vec_sb[:, i:i + 1] for i in range(5))
        tapcols = sb("tapcols", [P, 3, 32])
        zbias = sb("zbias", [P, 1])
        badap0 = sb("badap0", [P, 1])
        stats = sb("stats", [P, 2, THIRDS, 3])
        pooled = sb("pooled", [P, 2, TAPS + 1])
        fbias = sb("fbias", [P, 2])
        gates = sb("gates", [P, 2, TAPS])
        sm = sb("sm", [P, 24])
        var_eps = sb("var_eps", [P, 1])

        ab_ps = [ctx.enter_context(nc.psum_tensor(f"ab_ps{i}", [P, BANK], f32)) for i in range(3)]
        c_ps = [ctx.enter_context(nc.psum_tensor(f"c_ps{i}", [P, 2, BANK], f32)) for i in range(2)]
        small_ps = ctx.enter_context(nc.psum_tensor("small_ps", [P, BANK], f32))
        mean_ps, var_ps = small_ps[:, 0:1], small_ps[:, 1:2]
        gate_ps = small_ps[:, 2:2 + TAPS + 1]
        zb_ps = small_ps[:, 16:17]

        w_loaded = sem("w_loaded")
        wf_zeroed = sem("wf_zeroed")
        wf_loaded = sem("wf_loaded")
        tapcols_zeroed = sem("tapcols_zeroed")
        ready_dve = sem("ready_dve")
        ready_pool = sem("ready_pool")
        zb_summed = sem("zb_summed")
        x_loaded = [[sem(f"x_loaded{b}{t}") for t in range(THIRDS)] for b in range(NX)]
        x_stored = [[sem(f"x_stored{b}{t}") for t in range(THIRDS)] for b in range(NX)]
        pairs_ready = sem("pairs_ready")
        squared = sem("squared")
        summed = sem("summed")
        maxed = sem("maxed")
        pool_step = sem("pool_step")
        mean_own = sem("mean_own")
        mean_summed = sem("mean_summed")
        mean_ready = sem("mean_ready")
        spread_own = sem("spread_own")
        var_summed = sem("var_summed")
        var_ready = sem("var_ready")
        fold_ready = sem("fold_ready")
        gates_summed = sem("gates_summed")
        fbias_ready = sem("fbias_ready")
        gates_ready = sem("gates_ready")
        tapsel_ready = sem("tapsel_ready")
        tapw_summed = sem("tapw_summed")
        tapw_head = sem("tapw_head")
        tapw_rest = sem("tapw_rest")
        ab_summed = sem("ab_summed")
        f_ready = sem("f_ready")
        edges_zeroed = sem("edges_zeroed")
        head_ready = sem("head_ready")
        fields_ready = sem("fields_ready")
        c_summed = sem("c_summed")
        c_added = sem("c_added")
        c_copied = sem("c_copied")
        c_pool_added = sem("c_pool_added")

        class Img:

            def __init__(self, it, k):
                self.it, self.k = it, k
                self.buf, self.par = k % NX, k % 2

            def __add__(self, d):
                return Img(self.it, self.k + d)

            def n(self, per, more):
                if isinstance(self.it, int):
                    return (NX * self.it + self.k) * per + more
                assert self.k * per + more > 0
                return self.it * (NX * per) + (self.k * per + more)

            def use(self, more):
                if isinstance(self.it, int):
                    return 16 * (self.it + self.k // NX + more)
                assert self.k // NX + more > 0
                return self.it * 16 + 16 * (self.k // NX + more)

            def dram(self, ap, t):
                if isinstance(self.it, int):
                    return ap[NX * self.it + self.k, :, t * TPIX:(t + 1) * TPIX]
                return ap[bass.ds(self.it * NX + self.k, 1), :, t * TPIX:(t + 1) * TPIX].rearrange(
                    "o c w -> (o c) w")

        def wait(eng, s, value):
            if not isinstance(value, int) or value > 0:
                eng.wait_ge(s, value)

        def xt(img, t):
            return x_sb[:, img.buf, t * TPIX:(t + 1) * TPIX]

        def run_slots(eng, slot, first=2):
            trips = (N - 4) // NX
            for s in range(-2, first):
                slot(Img(0, s), s)
            with eng.Fori(0, trips) as it:
                for j in range(first, first + NX):
                    slot(Img(it, j), None)
            for s in range(first + trips * NX, N + 1):
                slot(Img(0, s), s)

        def has(s, d):
            return s is None or 0 <= s + d < N

        block = ctx.enter_context(nc.Block())

        @block.sync
        def _(sp):
            sp.dma_start(const_sb[:], const_d).then_inc(w_loaded, 16)
            sp.dma_start(vec_sb[:], vec_d).then_inc(w_loaded, 16)
            sp.dma_start(w1_sb[:], w1_d).then_inc(w_loaded, 16)

            def load(img, t):
                wait(sp, x_stored[img.buf][t], img.use(0))
                sp.dma_start(xt(img, t), img.dram(x_d, t)).then_inc(x_loaded[img.buf][t], 16)

            for n in range(2):
                for t in range(THIRDS):
                    load(Img(0, n), t)
                    if n == 0 and t == 0:
                        sp.wait_ge(wf_zeroed, 1)
                        for q in range(CHUNKS):
                            sp.dma_start(wf_sb[q * CM:(q + 1) * CM, q, :], wf_d).then_inc(wf_loaded, 16)

            def slot(img, s):
                if has(s, 3) and (s is None or s > -2):
                    for t in range(THIRDS):
                        load(img + 3, t)

            run_slots(sp, slot, first=1)
            for img in range(N - NX, N):
                for t in range(THIRDS):
                    sp.wait_ge(x_stored[img % NX][t], 16 * (img // NX + 1))

        @block.gpsimd
        def _(pool):
            nc.gpsimd.memset(f_sb[:], 0.0).then_inc(ready_pool, 1)
            pool.wait_ge(w_loaded, 48)
            pool.wait_ge(ready_pool, 1)
            nc.gpsimd.tensor_copy(tapsel[:], slotmask).then_inc(ready_pool, 1)
            nc.gpsimd.tensor_tensor(badap0[:], badap, badap_mask, ALU.mult).then_inc(ready_pool, 1)
            pool.wait_ge(ready_pool, 3)

            def pair(img, t):
                third = xt(img, t)
                wait(pool, x_loaded[img.buf][t], img.use(1))
                wait(pool, summed, img.n(THIRDS, t))
                nc.gpsimd.tensor_tensor(pairs[:], third[:, 0:TPIX // 2], third[:, TPIX // 2:TPIX],
                                        ALU.add).then_inc(pairs_ready, 1)

            STEPS = 15

            def then(ins, img, k):
                ins.then_inc(pool_step, 1)
                pool.wait_ge(pool_step, img.n(STEPS, k))

            def fold_means(img):
                st = stats[:, img.par]
                wait(pool, squared, img.n(6, 6))
                wait(pool, summed, img.n(THIRDS, THIRDS))
                then(nc.gpsimd.tensor_tensor(sm[:, 0:3], st[:, 0, :], st[:, 1, :], ALU.add), img, 1)
                then(nc.gpsimd.tensor_tensor(sm[:, 20:23], sm[:, 0:3], st[:, 2, :], ALU.add), img, 2)
                nc.gpsimd.tensor_tensor(sm[:, 4:5], sm[:, 20:21], per_pixel, ALU.mult).then_inc(mean_own, 1)
                then(nc.gpsimd.tensor_tensor(sm[:, 3:4], sm[:, 21:22], sm[:, 22:23], ALU.add), img, 3)
                pool.wait_ge(mean_own, img.n(1, 1))
                then(nc.gpsimd.tensor_tensor(sm[:, 5:6], sm[:, 3:4], per_pixel, ALU.mult), img, 4)
                then(nc.gpsimd.tensor_tensor(sm[:, 6:7], sm[:, 4:5], x_sb[:, img.buf, 0:1], ALU.subtract),
                     img, 5)
                then(nc.gpsimd.tensor_tensor(sm[:, 7:8], sm[:, 6:7], sm[:, 6:7], ALU.mult), img, 6)
                then(nc.gpsimd.tensor_tensor(sm[:, 8:9], sm[:, 5:6], sm[:, 7:8], ALU.subtract), img, 7)

            def fold_spread(img):
                pool.wait_ge(mean_ready, img.n(1, 1))
                then(nc.gpsimd.tensor_tensor(sm[:, 9:10], sm[:, 4:5], pooled[:, img.par, TAPS:TAPS + 1],
                                             ALU.subtract), img, 8)
                then(nc.gpsimd.tensor_tensor(sm[:, 10:11], sm[:, 9:10], sm[:, 9:10], ALU.mult), img, 9)
                nc.gpsimd.tensor_tensor(sm[:, 11:12], sm[:, 8:9], sm[:, 10:11], ALU.add
                                        ).then_inc(spread_own, 1)

            def fold_weights(img):
                pool.wait_ge(var_ready, img.n(1, 1))
                v, r0, rstd = var_eps[:], sm[:, 12:13], sm[:, 16:17]
                then(nc.gpsimd.tensor_tensor(r0, v, minus_half, ALU.pow), img, 10)
                then(nc.gpsimd.tensor_tensor(sm[:, 17:18], v, minus_half, ALU.mult), img, 11)
                then(nc.gpsimd.tensor_tensor(sm[:, 13:14], r0, r0, ALU.mult), img, 12)
                then(nc.gpsimd.tensor_tensor(sm[:, 14:15], sm[:, 13:14], sm[:, 17:18], ALU.mult), img, 13)
                then(nc.gpsimd.tensor_tensor(sm[:, 15:16], sm[:, 14:15], one_half_more, ALU.add), img, 14)
                then(nc.gpsimd.tensor_tensor(rstd, r0, sm[:, 15:16], ALU.mult), img, 15)
                wait(pool, ab_summed, (img + -2).n(NA + NB, NA))
                nc.gpsimd.tensor_tensor(w1_fold[:, img.par, :], w1_sb[:], rstd.to_broadcast([P, P]),
                                        ALU.mult).then_inc(fold_ready, 1)

            def place_gates(img):
                wait(pool, gates_ready, img.n(1, 1))
                wait(pool, tapw_summed, img.n(1, 0))
                g = gates[:, img.par, :]
                sel = tapsel[:, :].rearrange("p (c j r) -> p c j r", c=SETS, j=SLOTS)
                msk = slotmask.rearrange("p (c j r) -> p c j r", c=SETS, j=SLOTS)
                rows = 2 * CHUNKS
                nc.gpsimd.tensor_tensor(sel[:, :, 0:LAST, :], msk[:, :, 0:LAST, :],
                                        g[:, 0:TAPS - 1].rearrange("p (c j r) -> p c j r", c=SETS, r=1
                                                                   ).to_broadcast([P, SETS, LAST, rows]),
                                        ALU.mult).then_inc(tapsel_ready, 1)
                nc.gpsimd.tensor_tensor(sel[:, :, LAST, :], msk[:, :, LAST, :],
                                        g[:, TAPS - 1:TAPS].rearrange("p (c r) -> p c r", c=1
                                                                      ).to_broadcast([P, SETS, rows]),
                                        ALU.mult).then_inc(tapsel_ready, 1)

            def pool_add(img, k):
                u = POOL_ADDS[k]
                wait(pool, c_copied, img.n(len(POOL_ADDS), k + 1))
                part = x_sb[:, img.buf, u * CU:(u + 1) * CU].rearrange("p (b w) -> p b w", b=2)
                nc.gpsimd.tensor_tensor(part, z_sb[:], part, ALU.add).then_inc(c_pool_added, 1)

            def slot(img, s):
                done, fold, later = img + -1, img + 1, img + 2
                if has(s, 0):
                    place_gates(img)
                if has(s, 1):
                    pair(fold, 2)
                    fold_means(fold)
                if has(s, 2):
                    pair(later, 0)
                if has(s, 1):
                    fold_spread(fold)
                if has(s, -1):
                    pool_add(done, 0)
                if has(s, 1):
                    fold_weights(fold)
                if has(s, 2):
                    pair(later, 1)
                if has(s, -1):
                    pool_add(done, 1)

            run_slots(pool, slot)

        @block.scalar
        def _(act):
            act.wait_ge(ready_dve, 3)
            act.wait_ge(ready_pool, 1)

            def square(img, t, h):
                if h == 0:
                    wait(act, x_loaded[img.buf][t], img.use(1))
                wait(act, squared, img.n(2 * THIRDS, 2 * t + h))
                half = xt(img, t)[:, h * (TPIX // 2):(h + 1) * (TPIX // 2)]
                nc.scalar.activation(squares[:], half, ACT.Square, bias=x_sb[:, img.buf, 0:1], scale=-1.0,
                                     accum_out=stats[:, img.par, t, 1 + h:2 + h]).then_inc(squared, 1)

            def total(img, t):
                act.wait_ge(pairs_ready, img.n(THIRDS, t + 1))
                nc.scalar.activation(pairs[:], pairs[:], ACT.Copy,
                                     accum_out=stats[:, img.par, t, 0:1]).then_inc(summed, 1)

            def take_f(img, u):
                r, n = AUNITS[u]
                if u == 0:
                    act.wait_ge(fbias_ready, img.n(1, 1))
                act.wait_ge(ab_summed, img.n(NA + NB, u + 1))
                nc.scalar.activation(f_sb[:, r:r + n, 1:1 + WID],
                                     ab_ps[u % 3][:, 0:n * WID].rearrange("p (r w) -> p r w", w=WID),
                                     ACT.Relu, bias=fbias[:, img.par:img.par + 1]).then_inc(f_ready, 1)

            def head(img, u):
                act.wait_ge(ab_summed, img.n(NA + NB, NA + u + 1))
                wait(act, fields_ready, img.n(NB, u - 1))
                nc.scalar.activation(heads[u % 2][:], ab_ps[(NA + u) % 3][:, 0:BPIX],
                                     ACT.Copy).then_inc(head_ready, 1)

            def copy_c(img, k):
                u = POOL_ADDS[k]
                act.wait_ge(c_summed, img.n(NC, u + 1))
                wait(act, c_pool_added, img.n(len(POOL_ADDS), k))
                nc.scalar.activation(z_sb[:], c_ps[(img.k + u) % 2][:], ACT.Identity,
                                     bias=zbias[:]).then_inc(c_copied, 1)

            def store(img, t):
                u = NC // THIRDS * (t + 1)
                if u > dve_adds(u):
                    wait(act, c_pool_added, img.n(len(POOL_ADDS), u - dve_adds(u)))
                wait(act, c_added, img.n(dve_adds(NC), dve_adds(u)))
                act.dma_start(img.dram(out_d, t), xt(img, t)).then_inc(x_stored[img.buf][t], 16)

            def tap_head(img):
                act.wait_ge(tapw_summed, img.n(1, 1))
                nc.scalar.activation(tapw[img.par][HEAD][:], small_ps[:], ACT.Copy).then_inc(tapw_head, 1)

            def slot(img, s):
                done, later = img + -1, img + 2

                def takes(us):
                    if has(s, 0):
                        for u in us:
                            take_f(img, u)

                def heads_of(u):
                    if has(s, 0):
                        head(img, u)

                def squares_of(t, h):
                    if has(s, 1 if t == 2 else 2):
                        square(img + 1 if t == 2 else later, t, h)

                def totals(t):
                    if has(s, 1 if t == 2 else 2):
                        total(img + 1 if t == 2 else later, t)

                def copies(k):
                    if has(s, -1):
                        copy_c(done, k)

                def stores(t):
                    if has(s, -1):
                        store(done, t)

                takes([0])
                squares_of(2, 0)
                takes([1])
                squares_of(2, 1)
                takes([2, 3])
                totals(2)
                takes([4, 5])
                stores(0)
                if has(s, 0):
                    tap_head(img)
                heads_of(0)
                copies(0)
                squares_of(0, 0)
                heads_of(1)
                squares_of(0, 1)
                heads_of(2)
                stores(1)
                totals(0)
                heads_of(3)
                squares_of(1, 0)
                copies(1)
                heads_of(4)
                squares_of(1, 1)
                heads_of(5)
                stores(2)
                totals(1)

            run_slots(act, slot)

        @block.vector
        def _(dve):
            nc.vector.memset(wf_sb[:], 0.0).then_inc(wf_zeroed, 1)
            nc.vector.memset(tapcols[:], 0.0).then_inc(tapcols_zeroed, 1)
            for bank in ab_ps:
                last = nc.vector.memset(bank[:], 0.0)
            last.then_inc(ready_dve, 1)
            dve.wait_ge(w_loaded, 48)
            dve.wait_ge(tapcols_zeroed, 1)
            cols = tapcols[:, :, :].rearrange("p j (l q h) -> p j l q h", l=SLOTS, q=CHUNKS)
            for j in range(3):
                for q in range(CHUNKS):
                    rows = slice(q * CM, (q + 1) * CM)
                    nc.vector.tensor_copy(cols[rows, j, j, q, :], vec_sb[rows, 1:2].to_broadcast([CM, 2]))
                    last = nc.vector.tensor_copy(cols[rows, j, TSLOT, q, :],
                                                 vec_sb[rows, 2:3].to_broadcast([CM, 2]))
            last.then_inc(ready_dve, 1)
            dve.wait_ge(zb_summed, 1)
            nc.vector.tensor_tensor(zbias[:], zb_ps, bfuse, ALU.add).then_inc(ready_dve, 1)
            dve.wait_ge(ready_dve, 3)

            def block_max(img, k):
                t, a = k // 3, k % 3
                if a == 0:
                    wait(dve, x_loaded[img.buf][t], img.use(1))
                if k == 0:
                    wait(dve, gates_summed, img.n(1, -1))
                blocks = xt(img, t).rearrange("p (h a w) -> p h a w", h=BLK, a=3)
                nc.vector.tensor_reduce(pooled[:, img.par, k:k + 1], blocks[:, :, a, :],
                                        AX.XY, ALU.max).then_inc(maxed, 1)

            def zero_edge(img, first):
                dve.wait_ge(f_ready, img.n(NA, 1 if first else NA))
                edge = f_sb[0:CM, 0, 1:1 + WID] if first else f_sb[P - CM:P, FROWS - 1, 1:1 + WID]
                nc.vector.memset(edge, 0.0).then_inc(edges_zeroed, 1)

            def take_mean(img):
                dve.wait_ge(mean_summed, img.n(1, 1))
                nc.vector.tensor_copy(pooled[:, img.par, TAPS:TAPS + 1], mean_ps).then_inc(mean_ready, 1)

            def take_var(img):
                dve.wait_ge(var_summed, img.n(1, 1))
                nc.vector.tensor_scalar(var_eps[:], var_ps, EPS, None, ALU.add).then_inc(var_ready, 1)

            def take_gates(img):
                bias = fbias[:, img.par:img.par + 1]
                dve.wait_ge(gates_summed, img.n(1, 1))
                nc.vector.scalar_tensor_tensor(bias, gate_ps[:, TAPS:TAPS + 1], -1.0, b1, ALU.mult,
                                               ALU.add).then_inc(fbias_ready, 1)
                dve.wait_ge(fbias_ready, img.n(1, 1))
                wait(dve, tapsel_ready, (img + -2).n(2, 2))
                nc.vector.tensor_scalar(gates[:, img.par, :], gate_ps[:, 0:TAPS], bias, 0.0, ALU.add,
                                        ALU.max).then_inc(gates_ready, 1)

            def tap_rest(img):
                dve.wait_ge(tapw_head, img.n(1, 1))
                nc.vector.tensor_tensor(tapw[img.par][REST][:], small_ps[:], tapw[img.par][HEAD][:],
                                        ALU.subtract).then_inc(tapw_rest, 1)

            def split(img, u):
                dve.wait_ge(head_ready, img.n(NB, u + 1))
                nc.vector.scalar_tensor_tensor(fields[img.par][:, u * BPIX:(u + 1) * BPIX], heads[u % 2][:],
                                               restmask, ab_ps[(NA + u) % 3][:, 0:BPIX], ALU.mult,
                                               ALU.add).then_inc(fields_ready, 1)

            def add(img, u):
                dve.wait_ge(c_summed, img.n(NC, u + 1))
                part = x_sb[:, img.buf, u * CU:(u + 1) * CU].rearrange("p (b w) -> p b w", b=2)
                nc.vector.scalar_tensor_tensor(part, c_ps[(img.k + u) % 2][:], zbias[:], part, ALU.add,
                                               ALU.add).then_inc(c_added, 1)

            def slot(img, s):
                done, later = img + -1, img + 2

                def adds(us):
                    if has(s, -1):
                        for u in us:
                            add(done, u)

                def splits(u):
                    if has(s, 0):
                        split(img, u)

                def maxima(ks):
                    for k in ks:
                        if has(s, 1 if k >= 6 else 2):
                            block_max(img + 1 if k >= 6 else later, k)

                adds([0])
                if has(s, 0):
                    zero_edge(img, True)
                maxima([6])
                adds([1, 2])
                maxima([7])
                adds([3])
                maxima([8])
                if has(s, 0):
                    tap_rest(img)
                    zero_edge(img, False)
                splits(0)
                if has(s, 1):
                    take_mean(img + 1)
                maxima([0])
                splits(1)
                adds([5])
                maxima([1])
                if has(s, 1):
                    take_var(img + 1)
                splits(2)
                adds([6])
                maxima([2])
                splits(3)
                maxima([3])
                if has(s, 1):
                    take_gates(img + 1)
                splits(4)
                adds([8])
                maxima([4])
                splits(5)
                maxima([5])

            run_slots(dve, slot)

        @block.tensor
        def _(pe):
            pe.wait_ge(wf_loaded, 16 * CHUNKS)
            pe.wait_ge(ready_pool, 3)
            nc.tensor.matmul(zb_ps, wf_sb[:, 0, :], badap0[:], start=True, stop=True).then_inc(zb_summed, 1)
            pe.wait_ge(ready_dve, 3)

            def unit_free(img, u):
                if u >= 3 and u - 3 < NA:
                    pe.wait_ge(f_ready, img.n(NA, u - 2))
                elif u >= 3:
                    pe.wait_ge(fields_ready, img.n(NB, u - 2 - NA))
                else:
                    wait(pe, fields_ready, img.n(NB, u - 2))

            def conv_a(img, u):
                r, n = AUNITS[u]
                if u == 0:
                    pe.wait_ge(fold_ready, img.n(1, 1))
                unit_free(img, u)
                for q in range(CHUNKS):
                    lo, hi = max(CROWS * q + r - 1, 0), min(CROWS * q + r - 1 + n, HGT)
                    at = (lo - (CROWS * q + r - 1)) * WID
                    last = nc.tensor.matmul(ab_ps[u % 3][q * CM:(q + 1) * CM, at:at + (hi - lo) * WID],
                                            w1_fold[:, img.par, 0:CM], x_sb[:, img.buf, lo * WID:hi * WID],
                                            start=True, stop=True)
                last.then_inc(ab_summed, 1)

            def taps_b(img, u):
                unit_free(img, NA + u)
                pe.wait_ge(f_ready, img.n(NA, min(u + 2, NA)))
                if u == 0:
                    pe.wait_ge(edges_zeroed, img.n(2, 1))
                if u == NB - 1:
                    pe.wait_ge(edges_zeroed, img.n(2, 2))
                for j in range(3):
                    for c in range(SETS):
                        kh, kw = (2 * c + j) // 3, (2 * c + j) % 3
                        rows, first = BROWS, 0
                        if j == LAST:
                            kh, kw, rows, first = 2, 2, 1, c
                        at = BROWS * u + first + kh
                        last = nc.tensor.matmul(
                            ab_ps[(NA + u) % 3][32 * c:32 * c + 32, first * WID:(first + rows) * WID],
                            tapcols[:, j, :], f_sb[:, at:at + rows, kw:kw + WID],
                            start=(j == 0), stop=(j == LAST))
                last.then_inc(ab_summed, 1)

            def conv_c(img, u):
                if u == 0:
                    pe.wait_ge(fields_ready, img.n(NB, NB))
                    pe.wait_ge(tapw_rest, img.n(1, 1))
                if u - 2 in POOL_ADDS:
                    pe.wait_ge(c_copied, img.n(len(POOL_ADDS), POOL_ADDS.index(u - 2) + 1))
                elif u >= 2:
                    pe.wait_ge(c_added, img.n(dve_adds(NC), dve_adds(u - 1)))
                elif NC + u - 2 in POOL_ADDS:
                    wait(pe, c_copied, img.n(len(POOL_ADDS), 0))
                else:
                    wait(pe, c_added, img.n(dve_adds(NC), u - 1))
                for h in range(2):
                    a = u * CU + h * BANK
                    while a < u * CU + (h + 1) * BANK:
                        q = a // CPIX
                        b = min((q + 1) * CPIX, u * CU + (h + 1) * BANK)
                        o = a - u * CU - h * BANK
                        for part in (HEAD, REST):
                            last = nc.tensor.matmul(c_ps[(img.k + u) % 2][:, h, o:o + b - a],
                                                    tapw[img.par][part][:, q * P:(q + 1) * P],
                                                    fields[img.par][:, a - q * CPIX:b - q * CPIX],
                                                    start=(part == HEAD), stop=(part == REST))
                        a = b
                last.then_inc(c_summed, 1)

            def sum_mean(img):
                pe.wait_ge(mean_own, img.n(1, 1))
                wait(pe, gates_ready, img.n(1, 0))
                wait(pe, tapw_rest, img.n(1, 0))
                nc.tensor.matmul(mean_ps, group_avg, sm[:, 4:5], start=True, stop=True
                                 ).then_inc(mean_summed, 1)

            def sum_var(img):
                pe.wait_ge(spread_own, img.n(1, 1))
                nc.tensor.matmul(var_ps, group_avg, sm[:, 11:12], start=True, stop=True
                                 ).then_inc(var_summed, 1)

            def sum_gates(img):
                pe.wait_ge(fold_ready, img.n(1, 1))
                pe.wait_ge(maxed, img.n(THIRDS, THIRDS))
                nc.tensor.matmul(gate_ps, w1_fold[:, img.par, :], pooled[:, img.par, :], start=True,
                                 stop=True).then_inc(gates_summed, 1)

            def sum_tapw(img):
                pe.wait_ge(tapsel_ready, img.n(2, 2))
                nc.tensor.matmul(small_ps[:], tapsel[:], wf_sb[:, :, :].rearrange("p q o -> p (q o)"),
                                 start=True, stop=True).then_inc(tapw_summed, 1)

            def slot(img, s):
                done = img + -1

                def a(u):
                    if has(s, 0):
                        conv_a(img, u)

                def b(u):
                    if has(s, 0):
                        taps_b(img, u)

                def c(u):
                    if has(s, -1):
                        conv_c(done, u)

                a(0)
                a(1)
                c(0)
                a(2)
                c(1)
                a(3)
                c(2)
                a(4)
                c(3)
                a(5)
                if has(s, 0):
                    sum_tapw(img)
                b(0)
                c(4)
                if has(s, 1):
                    sum_mean(img + 1)
                b(1)
                c(5)
                b(2)
                if has(s, 1):
                    sum_var(img + 1)
                c(6)
                b(3)
                c(7)
                if has(s, 1):
                    sum_gates(img + 1)
                b(4)
                c(8)
                b(5)

            run_slots(pe, slot)


def constants():
    k = np.arange(P)
    out = np.zeros((P, 2 * P + 6), np.float32)
    out[:, 0:P] = (k[:, None] // GROUP == k[None, :] // GROUP) / GROUP
    for c in range(SETS):
        for j in range(SLOTS):
            for q in range(CHUNKS):
                at = P + 32 * c + 8 * j + 2 * q
                out[q * CM:(q + 1) * CM, at:at + 2] = 1.0
    out[:, 2 * P] = -(k % 2)
    out[:, 2 * P + 1] = -0.5
    out[:, 2 * P + 2] = k < CM
    out[:, 2 * P + 3] = 1.5
    out[:, 2 * P + 4:] = 1.0 / PIX
    return out


def kernel(x, L0_conv_w1, L0_conv_b1, L0_conv_wk, L0_conv_bk, L0_conv_b_adap, L0_conv_w_fuse,
           L0_conv_b_fuse):
    import concourse.bacc as _bacc
    from concourse.bass_utils import run_bass_kernel_spmd as _run

    rep = [np.tile(np.asarray(v), CHUNKS) for v in (L0_conv_b1, L0_conv_wk, L0_conv_bk, L0_conv_b_adap)]
    arrays = {
        "x_in": np.ascontiguousarray(x).reshape(N, C, PIX),
        "w1_in": np.ascontiguousarray(np.tile(np.asarray(L0_conv_w1).T, (1, CHUNKS))),
        "vec_in": np.ascontiguousarray(np.stack([*rep, np.asarray(L0_conv_b_fuse)], axis=1)),
        "wf_in": np.ascontiguousarray(np.asarray(L0_conv_w_fuse).T),
        "const_in": constants(),
    }
    nc = _bacc.Bacc("TRN2", target_bir_lowering=False, num_devices=1)
    aps = [nc.dram_tensor(n, a.shape, mybir.dt.from_np(a.dtype), kind="ExternalInput").ap()
           for n, a in arrays.items()]
    out = nc.dram_tensor("x_out", (N, C, PIX), mybir.dt.float32, kind="ExternalOutput").ap()
    conv_kernel(nc, *aps, out)
    r = _run(nc, [arrays], core_ids=[0])
    return r.results[0]["x_out"].reshape(N, C, HGT, WID)
```

```python
import numpy as np
import concourse.bass as bass
from concourse import mybir
from contextlib import ExitStack

N, C, HGT, WID = 32, 128, 96, 96
PIX = HGT * WID
CM = 32
P = 128
GROUP = C // 32
EPS = 1e-5
TAPS = 9
CHUNKS = P // CM
CROWS = HGT // CHUNKS
CPIX = CROWS * WID
FROWS, FW = CROWS + 2, WID + 2
THIRDS = 3
TPIX = PIX // THIRDS
BLK = HGT // 3
AUNITS = [(0, 5), (5, 4), (9, 4), (13, 4), (17, 4), (21, 5)]
NA = len(AUNITS)
BROWS = 4
NB = CROWS // BROWS
BPIX = BROWS * WID
BANK = 512
CU = 2 * BANK
NC = PIX // CU
NX = 4
SETS = P // 32
HEAD, REST = 0, 1


SLOTS = 4
LAST, TSLOT = 2, 3
POOL_ADDS = (4, 7)


def fields_needed(u):
    pixels = [p % CPIX for p in range(u * CU, (u + 1) * CU)]
    return max(pixels) // BPIX + 1


LAST_ORDER = sorted(range(NC), key=lambda u: fields_needed(u))
EARLY = 4
EARLY_STORES = 2


def dve_adds(u):
    return u - sum(v < u for v in POOL_ADDS)


def conv_kernel(nc, x_d, w1_d, vec_d, wf_d, const_d, out_d):
    f32, f32r, bf16 = mybir.dt.float32, mybir.dt.float32r, mybir.dt.bfloat16
    ALU, ACT, AX = mybir.AluOpType, mybir.ActivationFunctionType, mybir.AxisListType

    ctx = ExitStack()
    with ctx:
        def sb(name, shape, dt=f32):
            return ctx.enter_context(nc.sbuf_tensor(name, shape, dt))

        def sem(name):
            return ctx.enter_context(nc.semaphore(name))

        x_sb = sb("x_sb", [P, NX, PIX])
        f_sb = sb("f_sb", [P, FROWS, FW])
        fields = [sb(f"fields{i}", [P, CPIX], f32r) for i in range(2)]
        heads = [sb(f"heads{i}", [P, BPIX], f32r) for i in range(2)]
        z_sb = sb("z_sb", [P, 2, BANK])
        squares = sb("squares", [P, TPIX], bf16)
        pairs = sb("pairs", [P, TPIX // 2])
        tapw = [[sb(f"tapw{i}{h}", [P, CHUNKS * P], f32r) for h in range(2)] for i in range(2)]
        w1_sb = sb("w1_sb", [P, P])
        w1_fold = sb("w1_fold", [P, 2, P])
        wf_sb = sb("wf_sb", [P, CHUNKS, P])
        tapsel = sb("tapsel", [P, P])
        const_sb = sb("const_sb", [P, 2 * P + 6])
        group_avg = const_sb[:, 0:P]
        slotmask = const_sb[:, P:2 * P]
        restmask = const_sb[:, 2 * P:2 * P + 1]
        minus_half = const_sb[:, 2 * P + 1:2 * P + 2]
        badap_mask = const_sb[:, 2 * P + 2:2 * P + 3]
        one_half_more = const_sb[:, 2 * P + 3:2 * P + 4]
        per_pixel = const_sb[:, 2 * P + 4:2 * P + 5]
        vec_sb = sb("vec_sb", [P, 5])
        b1, wk, bk, badap, bfuse = (vec_sb[:, i:i + 1] for i in range(5))
        tapcols = sb("tapcols", [P, 3, 32])
        zbias = sb("zbias", [P, 1])
        badap0 = sb("badap0", [P, 1])
        stats = sb("stats", [P, 2, THIRDS, 3])
        pooled = sb("pooled", [P, 2, TAPS + 1])
        fbias = sb("fbias", [P, 2])
        gates = sb("gates", [P, 2, TAPS])
        warm = sb("warm", [P, 1])
        sm = sb("sm", [P, 24])
        var_eps = sb("var_eps", [P, 1])

        ab_ps = [ctx.enter_context(nc.psum_tensor(f"ab_ps{i}", [P, BANK], f32)) for i in range(3)]
        c_ps = [ctx.enter_context(nc.psum_tensor(f"c_ps{i}", [P, 2, BANK], f32)) for i in range(2)]
        small_ps = ctx.enter_context(nc.psum_tensor("small_ps", [P, BANK], f32))
        mean_ps, var_ps = small_ps[:, 0:1], small_ps[:, 1:2]
        gate_ps = small_ps[:, 2:2 + TAPS + 1]
        zb_ps = small_ps[:, 16:17]

        w_loaded = sem("w_loaded")
        warm_zeroed = sem("warm_zeroed")
        wf_zeroed = sem("wf_zeroed")
        wf_loaded = sem("wf_loaded")
        tapcols_zeroed = sem("tapcols_zeroed")
        ready_dve = sem("ready_dve")
        ready_pool = sem("ready_pool")
        zb_summed = sem("zb_summed")
        x_loaded = [[sem(f"x_loaded{b}{t}") for t in range(THIRDS)] for b in range(NX)]
        x_stored = [[sem(f"x_stored{b}{t}") for t in range(THIRDS)] for b in range(NX)]
        last_stored = sem("last_stored")
        pairs_ready = sem("pairs_ready")
        squared = sem("squared")
        summed = sem("summed")
        maxed = sem("maxed")
        pool_step = sem("pool_step")
        mean_own = sem("mean_own")
        mean_summed = sem("mean_summed")
        mean_ready = sem("mean_ready")
        spread_own = sem("spread_own")
        var_summed = sem("var_summed")
        var_ready = sem("var_ready")
        fold_ready = sem("fold_ready")
        gates_summed = sem("gates_summed")
        fbias_ready = sem("fbias_ready")
        gates_ready = sem("gates_ready")
        tapsel_ready = sem("tapsel_ready")
        tapw_summed = sem("tapw_summed")
        tapw_head = sem("tapw_head")
        tapw_rest = sem("tapw_rest")
        ab_summed = sem("ab_summed")
        f_ready = sem("f_ready")
        edges_zeroed = sem("edges_zeroed")
        head_ready = sem("head_ready")
        fields_ready = sem("fields_ready")
        c_summed = sem("c_summed")
        c_added = sem("c_added")
        c_copied = sem("c_copied")
        c_pool_added = sem("c_pool_added")

        class Img:

            def __init__(self, it, k):
                self.it, self.k = it, k
                self.buf, self.par = k % NX, k % 2

            def __add__(self, d):
                return Img(self.it, self.k + d)

            def n(self, per, more):
                if isinstance(self.it, int):
                    return (NX * self.it + self.k) * per + more
                assert self.k * per + more > 0
                return self.it * (NX * per) + (self.k * per + more)

            def is_last(self):
                return isinstance(self.it, int) and self.k == N - 1

            def c_unit(self, i):
                return LAST_ORDER[i] if self.is_last() else i

            def alone(self):
                return isinstance(self.it, int) and self.k in (2, 3)

            def pairs(self, t):
                skipped = min(max(self.k - 1, 0), 2) if isinstance(self.it, int) else 2
                return self.n(THIRDS, t + 1 - skipped)

            def use(self, more):
                if isinstance(self.it, int):
                    return 16 * (self.it + self.k // NX + more)
                assert self.k // NX + more > 0
                return self.it * 16 + 16 * (self.k // NX + more)

            def dram(self, ap, t):
                if isinstance(self.it, int):
                    return ap[NX * self.it + self.k, :, t * TPIX:(t + 1) * TPIX]
                return ap[bass.ds(self.it * NX + self.k, 1), :, t * TPIX:(t + 1) * TPIX].rearrange(
                    "o c w -> (o c) w")

        def wait(eng, s, value):
            if not isinstance(value, int) or value > 0:
                eng.wait_ge(s, value)

        def xt(img, t):
            return x_sb[:, img.buf, t * TPIX:(t + 1) * TPIX]

        def run_slots(eng, slot, first=2):
            trips = (N - 4) // NX
            for s in range(-2, first):
                slot(Img(0, s), s)
            with eng.Fori(0, trips) as it:
                for j in range(first, first + NX):
                    slot(Img(it, j), None)
            for s in range(first + trips * NX, N + 1):
                slot(Img(0, s), s)

        def has(s, d):
            return s is None or 0 <= s + d < N

        block = ctx.enter_context(nc.Block())

        @block.sync
        def _(sp):
            def load(img, t):
                wait(sp, x_stored[img.buf][t], img.use(0))
                sp.dma_start(xt(img, t), img.dram(x_d, t)).then_inc(x_loaded[img.buf][t], 16)

            for n in range(2):
                for t in range(THIRDS):
                    load(Img(0, n), t)
                if n == 0:
                    sp.dma_start(const_sb[:], const_d).then_inc(w_loaded, 16)
                    sp.dma_start(vec_sb[:], vec_d).then_inc(w_loaded, 16)
                    sp.dma_start(w1_sb[:], w1_d).then_inc(w_loaded, 16)
                    sp.wait_ge(wf_zeroed, 1)
                    for q in range(CHUNKS):
                        sp.dma_start(wf_sb[q * CM:(q + 1) * CM, q, :], wf_d).then_inc(wf_loaded, 16)

            def slot(img, s):
                if has(s, 3) and (s is None or s > -2):
                    for t in range(THIRDS):
                        load(img + 3, t)

            run_slots(sp, slot, first=1)
            for img in range(N - NX, N - 1):
                for t in range(THIRDS):
                    sp.wait_ge(x_stored[img % NX][t], 16 * (img // NX + 1))
            sp.wait_ge(last_stored, 16 * NC)

        @block.gpsimd
        def _(pool):
            nc.gpsimd.memset(f_sb[:], 0.0).then_inc(ready_pool, 1)

            def pair(img, t):
                third = xt(img, t)
                wait(pool, x_loaded[img.buf][t], img.use(1))
                before = 0 if img.alone() and t == 1 else t
                wait(pool, summed, img.n(THIRDS, before))
                nc.gpsimd.tensor_tensor(pairs[:], third[:, 0:TPIX // 2], third[:, TPIX // 2:TPIX],
                                        ALU.add).then_inc(pairs_ready, 1)

            STEPS = 15

            def then(ins, img, k):
                ins.then_inc(pool_step, 1)
                pool.wait_ge(pool_step, img.n(STEPS, k))

            def fold_means(img):
                st = stats[:, img.par]
                wait(pool, squared, img.n(6, 6))
                wait(pool, summed, img.n(THIRDS, THIRDS))
                then(nc.gpsimd.tensor_tensor(sm[:, 0:3], st[:, 0, :], st[:, 1, :], ALU.add), img, 1)
                then(nc.gpsimd.tensor_tensor(sm[:, 20:23], sm[:, 0:3], st[:, 2, :], ALU.add), img, 2)
                nc.gpsimd.tensor_tensor(sm[:, 4:5], sm[:, 20:21], per_pixel, ALU.mult).then_inc(mean_own, 1)
                then(nc.gpsimd.tensor_tensor(sm[:, 3:4], sm[:, 21:22], sm[:, 22:23], ALU.add), img, 3)
                pool.wait_ge(mean_own, img.n(1, 1))
                then(nc.gpsimd.tensor_tensor(sm[:, 5:6], sm[:, 3:4], per_pixel, ALU.mult), img, 4)
                then(nc.gpsimd.tensor_tensor(sm[:, 6:7], sm[:, 4:5], x_sb[:, img.buf, 0:1], ALU.subtract),
                     img, 5)
                then(nc.gpsimd.tensor_tensor(sm[:, 7:8], sm[:, 6:7], sm[:, 6:7], ALU.mult), img, 6)
                then(nc.gpsimd.tensor_tensor(sm[:, 8:9], sm[:, 5:6], sm[:, 7:8], ALU.subtract), img, 7)

            def fold_spread(img):
                pool.wait_ge(mean_ready, img.n(1, 1))
                then(nc.gpsimd.tensor_tensor(sm[:, 9:10], sm[:, 4:5], pooled[:, img.par, TAPS:TAPS + 1],
                                             ALU.subtract), img, 8)
                then(nc.gpsimd.tensor_tensor(sm[:, 10:11], sm[:, 9:10], sm[:, 9:10], ALU.mult), img, 9)
                nc.gpsimd.tensor_tensor(sm[:, 11:12], sm[:, 8:9], sm[:, 10:11], ALU.add
                                        ).then_inc(spread_own, 1)

            def fold_weights(img):
                pool.wait_ge(var_ready, img.n(1, 1))
                v, r0, rstd = var_eps[:], sm[:, 12:13], sm[:, 16:17]
                then(nc.gpsimd.tensor_tensor(r0, v, minus_half, ALU.pow), img, 10)
                then(nc.gpsimd.tensor_tensor(sm[:, 17:18], v, minus_half, ALU.mult), img, 11)
                then(nc.gpsimd.tensor_tensor(sm[:, 13:14], r0, r0, ALU.mult), img, 12)
                then(nc.gpsimd.tensor_tensor(sm[:, 14:15], sm[:, 13:14], sm[:, 17:18], ALU.mult), img, 13)
                then(nc.gpsimd.tensor_tensor(sm[:, 15:16], sm[:, 14:15], one_half_more, ALU.add), img, 14)
                then(nc.gpsimd.tensor_tensor(rstd, r0, sm[:, 15:16], ALU.mult), img, 15)
                wait(pool, ab_summed, (img + -2).n(NA + NB, NA))
                nc.gpsimd.tensor_tensor(w1_fold[:, img.par, :], w1_sb[:], rstd.to_broadcast([P, P]),
                                        ALU.mult).then_inc(fold_ready, 1)

            def place_gates(img):
                wait(pool, gates_ready, img.n(1, 1))
                wait(pool, tapw_summed, img.n(1, 0))
                g = gates[:, img.par, :]
                sel = tapsel[:, :].rearrange("p (c j r) -> p c j r", c=SETS, j=SLOTS)
                msk = slotmask.rearrange("p (c j r) -> p c j r", c=SETS, j=SLOTS)
                rows = 2 * CHUNKS
                nc.gpsimd.tensor_tensor(sel[:, :, 0:LAST, :], msk[:, :, 0:LAST, :],
                                        g[:, 0:TAPS - 1].rearrange("p (c j r) -> p c j r", c=SETS, r=1
                                                                   ).to_broadcast([P, SETS, LAST, rows]),
                                        ALU.mult).then_inc(tapsel_ready, 1)
                nc.gpsimd.tensor_tensor(sel[:, :, LAST, :], msk[:, :, LAST, :],
                                        g[:, TAPS - 1:TAPS].rearrange("p (c r) -> p c r", c=1
                                                                      ).to_broadcast([P, SETS, rows]),
                                        ALU.mult).then_inc(tapsel_ready, 1)

            def pool_add(img, k):
                u = POOL_ADDS[k]
                wait(pool, c_copied, img.n(len(POOL_ADDS), k + 1))
                part = x_sb[:, img.buf, u * CU:(u + 1) * CU].rearrange("p (b w) -> p b w", b=2)
                nc.gpsimd.tensor_tensor(part, z_sb[:], part, ALU.add).then_inc(c_pool_added, 1)

            def slot(img, s):
                done, fold, later = img + -1, img + 1, img + 2
                if s == N:
                    return
                if s == -1:
                    pair(fold, 2)
                    pool.wait_ge(w_loaded, 48)
                    nc.gpsimd.tensor_tensor(badap0[:], badap, badap_mask, ALU.mult).then_inc(ready_pool, 1)
                    fold_means(fold)
                    fold_spread(fold)
                    fold_weights(fold)
                    nc.gpsimd.tensor_copy(tapsel[:], slotmask).then_inc(ready_pool, 1)
                    pool.wait_ge(ready_pool, 3)
                    pair(later, 0)
                    pair(later, 1)
                    return
                if has(s, 0):
                    place_gates(img)
                if s == 0:
                    pair(fold, 2)
                    fold_means(fold)
                    fold_spread(fold)
                    fold_weights(fold)
                    pair(later, 1)
                    return
                if s == 1:
                    pair(fold, 2)
                    pool_add(done, 0)
                    fold_means(fold)
                    fold_spread(fold)
                    pair(later, 1)
                    fold_weights(fold)
                    pool_add(done, 1)
                    return
                if has(s, 1):
                    pair(fold, 2)
                    fold_means(fold)
                if has(s, 2):
                    pair(later, 0)
                if has(s, 1):
                    fold_spread(fold)
                if has(s, -1):
                    pool_add(done, 0)
                if has(s, 1):
                    fold_weights(fold)
                if has(s, 2):
                    pair(later, 1)
                if has(s, -1):
                    pool_add(done, 1)

            run_slots(pool, slot)

        @block.scalar
        def _(act):
            act.wait_ge(warm_zeroed, 1)
            nc.scalar.activation(warm[:], warm[:], ACT.Square)

            def square(img, t, h):
                if h == 0:
                    wait(act, x_loaded[img.buf][t], img.use(1))
                wait(act, squared, img.n(2 * THIRDS, 2 * t + h))
                half = xt(img, t)[:, h * (TPIX // 2):(h + 1) * (TPIX // 2)]
                nc.scalar.activation(squares[:, 0:TPIX // 2], half, ACT.Square,
                                     bias=x_sb[:, img.buf, 0:1], scale=-1.0,
                                     accum_out=stats[:, img.par, t, 1 + h:2 + h]).then_inc(squared, 1)

            def total_whole(img, t):
                act.wait_ge(x_loaded[img.buf][t], img.use(1))
                wait(act, squared, img.n(2 * THIRDS, 0))
                nc.scalar.activation(squares[:], xt(img, t), ACT.Copy,
                                     accum_out=stats[:, img.par, t, 0:1]).then_inc(summed, 1)

            def total(img, t):
                act.wait_ge(pairs_ready, img.pairs(t))
                nc.scalar.activation(pairs[:], pairs[:], ACT.Copy,
                                     accum_out=stats[:, img.par, t, 0:1]).then_inc(summed, 1)

            def take_f(img, u):
                r, n = AUNITS[u]
                if u == 0:
                    act.wait_ge(fbias_ready, img.n(1, 1))
                act.wait_ge(ab_summed, img.n(NA + NB, u + 1))
                nc.scalar.activation(f_sb[:, r:r + n, 1:1 + WID],
                                     ab_ps[u % 3][:, 0:n * WID].rearrange("p (r w) -> p r w", w=WID),
                                     ACT.Relu, bias=fbias[:, img.par:img.par + 1]).then_inc(f_ready, 1)

            def head(img, u):
                act.wait_ge(ab_summed, img.n(NA + NB, NA + u + 1))
                wait(act, fields_ready, img.n(NB, u - 1))
                nc.scalar.activation(heads[u % 2][:], ab_ps[(NA + u) % 3][:, 0:BPIX],
                                     ACT.Copy).then_inc(head_ready, 1)

            def copy_c(img, k):
                u = POOL_ADDS[k]
                act.wait_ge(c_summed, img.n(NC, u + 1))
                wait(act, c_pool_added, img.n(len(POOL_ADDS), k))
                nc.scalar.activation(z_sb[:], c_ps[(img.k + u) % 2][:], ACT.Identity,
                                     bias=zbias[:]).then_inc(c_copied, 1)

            def store(img, t):
                u = NC // THIRDS * (t + 1)
                if u > dve_adds(u):
                    wait(act, c_pool_added, img.n(len(POOL_ADDS), u - dve_adds(u)))
                wait(act, c_added, img.n(dve_adds(NC), dve_adds(u)))
                act.dma_start(img.dram(out_d, t), xt(img, t)).then_inc(x_stored[img.buf][t], 16)

            def store_unit(img, i):
                act.wait_ge(c_added, img.n(dve_adds(NC), i + 1))
                at = slice(img.c_unit(i) * CU, (img.c_unit(i) + 1) * CU)
                act.dma_start(out_d[N - 1, :, at], x_sb[:, img.buf, at]).then_inc(last_stored, 16)

            def tap_head(img):
                act.wait_ge(tapw_summed, img.n(1, 1))
                nc.scalar.activation(tapw[img.par][HEAD][:], small_ps[:], ACT.Copy).then_inc(tapw_head, 1)

            def slot(img, s):
                done, later = img + -1, img + 2

                def takes(us):
                    if has(s, 0):
                        for u in us:
                            take_f(img, u)

                def heads_of(u):
                    if has(s, 0):
                        head(img, u)

                def squares_of(t, h):
                    if has(s, 1 if t == 2 else 2):
                        square(img + 1 if t == 2 else later, t, h)

                def totals(t):
                    if has(s, 1 if t == 2 else 2):
                        total(img + 1 if t == 2 else later, t)

                def copies(k):
                    if has(s, -1):
                        copy_c(done, k)

                def stores(t):
                    if has(s, -1):
                        store(done, t)

                if s == N:
                    for i in range(EARLY_STORES, NC):
                        store_unit(done, i)
                    return
                if s == N - 1:
                    takes(range(NA))
                    stores(0)
                    copies(0)
                    tap_head(img)
                    heads_of(0)
                    stores(1)
                    heads_of(1)
                    copies(1)
                    heads_of(2)
                    heads_of(3)
                    stores(2)
                    heads_of(4)
                    for i in range(EARLY_STORES):
                        store_unit(img, i)
                    heads_of(5)
                    return

                if s == -1:
                    squares_of(2, 0)
                    squares_of(2, 1)
                    totals(2)
                    for t in (0, 1):
                        squares_of(t, 0)
                        squares_of(t, 1)
                    return
                if s == 0:
                    act.wait_ge(ready_dve, 3)
                    act.wait_ge(ready_pool, 1)
                    takes([0, 1])
                    total(img + 1, 0)
                    takes([2, 3])
                    squares_of(2, 0)
                    takes([4])
                    total(img + 1, 1)
                    takes([5])
                    tap_head(img)
                    squares_of(2, 1)
                    heads_of(0)
                    totals(2)
                    heads_of(1)
                    heads_of(2)
                    heads_of(3)
                    total_whole(later, 0)
                    heads_of(4)
                    act.wait_ge(summed, later.n(THIRDS, 1))
                    squares_of(0, 0)
                    heads_of(5)
                    squares_of(0, 1)
                    return
                if s == 1:
                    takes([0, 1, 2])
                    square(img + 1, 1, 0)
                    takes([3])
                    total(img + 1, 1)
                    takes([4])
                    square(img + 1, 1, 1)
                    takes([5])
                    stores(0)
                    squares_of(2, 0)
                    tap_head(img)
                    heads_of(0)
                    copies(0)
                    squares_of(2, 1)
                    totals(2)
                    heads_of(1)
                    total_whole(later, 0)
                    heads_of(2)
                    stores(1)
                    act.wait_ge(summed, later.n(THIRDS, 1))
                    squares_of(0, 0)
                    heads_of(3)
                    copies(1)
                    squares_of(0, 1)
                    heads_of(4)
                    squares_of(1, 0)
                    heads_of(5)
                    totals(1)
                    squares_of(1, 1)
                    stores(2)
                    return
                takes([0])
                squares_of(2, 0)
                takes([1])
                squares_of(2, 1)
                takes([2, 3])
                totals(2)
                takes([4, 5])
                stores(0)
                if has(s, 0):
                    tap_head(img)
                heads_of(0)
                copies(0)
                squares_of(0, 0)
                heads_of(1)
                squares_of(0, 1)
                heads_of(2)
                stores(1)
                totals(0)
                heads_of(3)
                squares_of(1, 0)
                copies(1)
                heads_of(4)
                squares_of(1, 1)
                heads_of(5)
                stores(2)
                totals(1)

            run_slots(act, slot)

        @block.vector
        def _(dve):
            nc.vector.memset(warm[:], 0.0).then_inc(warm_zeroed, 1)
            nc.vector.memset(wf_sb[:], 0.0).then_inc(wf_zeroed, 1)
            nc.vector.memset(tapcols[:], 0.0).then_inc(tapcols_zeroed, 1)
            for bank in ab_ps:
                last = nc.vector.memset(bank[:], 0.0)
            last.then_inc(ready_dve, 1)

            def weights():
                dve.wait_ge(w_loaded, 48)
                dve.wait_ge(tapcols_zeroed, 1)
                cols = tapcols[:, :, :].rearrange("p j (l q h) -> p j l q h", l=SLOTS, q=CHUNKS)
                for j in range(3):
                    for q in range(CHUNKS):
                        rows = slice(q * CM, (q + 1) * CM)
                        nc.vector.tensor_copy(cols[rows, j, j, q, :], vec_sb[rows, 1:2].to_broadcast([CM, 2]))
                        last = nc.vector.tensor_copy(cols[rows, j, TSLOT, q, :],
                                                     vec_sb[rows, 2:3].to_broadcast([CM, 2]))
                last.then_inc(ready_dve, 1)
                dve.wait_ge(zb_summed, 1)
                nc.vector.tensor_tensor(zbias[:], zb_ps, bfuse, ALU.add).then_inc(ready_dve, 1)
                dve.wait_ge(ready_dve, 3)

            def block_max(img, k):
                t, a = k // 3, k % 3
                if a == 0:
                    wait(dve, x_loaded[img.buf][t], img.use(1))
                if k == 0:
                    wait(dve, gates_summed, img.n(1, -1))
                blocks = xt(img, t).rearrange("p (h a w) -> p h a w", h=BLK, a=3)
                nc.vector.tensor_reduce(pooled[:, img.par, k:k + 1], blocks[:, :, a, :],
                                        AX.XY, ALU.max).then_inc(maxed, 1)

            def zero_edge(img, first):
                dve.wait_ge(f_ready, img.n(NA, 1 if first else NA))
                edge = f_sb[0:CM, 0, 1:1 + WID] if first else f_sb[P - CM:P, FROWS - 1, 1:1 + WID]
                nc.vector.memset(edge, 0.0).then_inc(edges_zeroed, 1)

            def take_mean(img):
                dve.wait_ge(mean_summed, img.n(1, 1))
                nc.vector.tensor_copy(pooled[:, img.par, TAPS:TAPS + 1], mean_ps).then_inc(mean_ready, 1)

            def take_var(img):
                dve.wait_ge(var_summed, img.n(1, 1))
                nc.vector.tensor_scalar(var_eps[:], var_ps, EPS, None, ALU.add).then_inc(var_ready, 1)

            def take_gates(img):
                bias = fbias[:, img.par:img.par + 1]
                dve.wait_ge(gates_summed, img.n(1, 1))
                nc.vector.scalar_tensor_tensor(bias, gate_ps[:, TAPS:TAPS + 1], -1.0, b1, ALU.mult,
                                               ALU.add).then_inc(fbias_ready, 1)
                dve.wait_ge(fbias_ready, img.n(1, 1))
                wait(dve, tapsel_ready, (img + -2).n(2, 2))
                nc.vector.tensor_scalar(gates[:, img.par, :], gate_ps[:, 0:TAPS], bias, 0.0, ALU.add,
                                        ALU.max).then_inc(gates_ready, 1)

            def tap_rest(img):
                dve.wait_ge(tapw_head, img.n(1, 1))
                nc.vector.tensor_tensor(tapw[img.par][REST][:], small_ps[:], tapw[img.par][HEAD][:],
                                        ALU.subtract).then_inc(tapw_rest, 1)

            def split(img, u):
                dve.wait_ge(head_ready, img.n(NB, u + 1))
                nc.vector.scalar_tensor_tensor(fields[img.par][:, u * BPIX:(u + 1) * BPIX], heads[u % 2][:],
                                               restmask, ab_ps[(NA + u) % 3][:, 0:BPIX], ALU.mult,
                                               ALU.add).then_inc(fields_ready, 1)

            def add(img, i):
                u = img.c_unit(i)
                dve.wait_ge(c_summed, img.n(NC, i + 1))
                part = x_sb[:, img.buf, u * CU:(u + 1) * CU].rearrange("p (b w) -> p b w", b=2)
                nc.vector.scalar_tensor_tensor(part, c_ps[(img.k + i) % 2][:], zbias[:], part, ALU.add,
                                               ALU.add).then_inc(c_added, 1)

            def slot(img, s):
                done, later = img + -1, img + 2

                def adds(us):
                    if has(s, -1):
                        for u in us:
                            add(done, u)

                def splits(u):
                    if has(s, 0):
                        split(img, u)

                def maxima(ks):
                    for k in ks:
                        if has(s, 1 if k >= 6 else 2):
                            block_max(img + 1 if k >= 6 else later, k)

                if s == N:
                    adds(range(EARLY, NC))
                    return
                if s == N - 1:
                    adds([0])
                    zero_edge(img, True)
                    adds([1, 2, 3])
                    zero_edge(img, False)
                    adds([5])
                    tap_rest(img)
                    splits(0)
                    adds([6])
                    splits(1)
                    splits(2)
                    adds([8])
                    splits(3)
                    add(img, 0)
                    splits(4)
                    add(img, 1)
                    add(img, 2)
                    splits(5)
                    add(img, 3)
                    return
                if s == -1:
                    maxima([6, 7, 8])
                    weights()
                    take_mean(img + 1)
                    take_var(img + 1)
                    maxima([0, 1])
                    take_gates(img + 1)
                    maxima([2, 3, 4, 5])
                    return
                if s == 0:
                    zero_edge(img, True)
                    maxima([6, 7, 8])
                    tap_rest(img)
                    zero_edge(img, False)
                    splits(0)
                    maxima([0])
                    splits(1)
                    maxima([1])
                    splits(2)
                    take_mean(img + 1)
                    splits(3)
                    take_var(img + 1)
                    splits(4)
                    maxima([2])
                    splits(5)
                    take_gates(img + 1)
                    maxima([3])
                    return
                adds([0])
                if has(s, 0):
                    zero_edge(img, True)
                maxima([6])
                adds([1, 2])
                maxima([7])
                adds([3])
                maxima([8])
                if has(s, 0):
                    tap_rest(img)
                    zero_edge(img, False)
                splits(0)
                if s == 1:
                    block_max(img + 1, 4)
                    block_max(img + 1, 5)
                    splits(1)
                    adds([5])
                    maxima([0])
                    splits(2)
                    take_mean(img + 1)
                    adds([6])
                    maxima([1])
                    splits(3)
                    maxima([2])
                    splits(4)
                    take_var(img + 1)
                    adds([8])
                    maxima([3])
                    splits(5)
                    take_gates(img + 1)
                    maxima([4, 5])
                    return
                if has(s, 1):
                    take_mean(img + 1)
                maxima([0])
                splits(1)
                adds([5])
                maxima([1])
                if has(s, 1):
                    take_var(img + 1)
                splits(2)
                adds([6])
                maxima([2])
                splits(3)
                maxima([3])
                if has(s, 1):
                    take_gates(img + 1)
                splits(4)
                adds([8])
                maxima([4])
                splits(5)
                maxima([5])

            run_slots(dve, slot)

        @block.tensor
        def _(pe):
            def bias_product():
                pe.wait_ge(wf_loaded, 16 * CHUNKS)
                pe.wait_ge(ready_pool, 2)
                nc.tensor.matmul(zb_ps, wf_sb[:, 0, :], badap0[:], start=True, stop=True
                                 ).then_inc(zb_summed, 1)
                pe.wait_ge(ready_dve, 3)

            def unit_free(img, u):
                if u >= 3 and u - 3 < NA:
                    pe.wait_ge(f_ready, img.n(NA, u - 2))
                elif u >= 3:
                    pe.wait_ge(fields_ready, img.n(NB, u - 2 - NA))
                else:
                    wait(pe, fields_ready, img.n(NB, u - 2))

            def conv_a(img, u):
                r, n = AUNITS[u]
                if u == 0:
                    pe.wait_ge(fold_ready, img.n(1, 1))
                unit_free(img, u)
                for q in range(CHUNKS):
                    lo, hi = max(CROWS * q + r - 1, 0), min(CROWS * q + r - 1 + n, HGT)
                    at = (lo - (CROWS * q + r - 1)) * WID
                    last = nc.tensor.matmul(ab_ps[u % 3][q * CM:(q + 1) * CM, at:at + (hi - lo) * WID],
                                            w1_fold[:, img.par, 0:CM], x_sb[:, img.buf, lo * WID:hi * WID],
                                            start=True, stop=True)
                last.then_inc(ab_summed, 1)

            def taps_b(img, u):
                unit_free(img, NA + u)
                pe.wait_ge(f_ready, img.n(NA, min(u + 2, NA)))
                if u == 0:
                    pe.wait_ge(edges_zeroed, img.n(2, 1))
                if u == NB - 1:
                    pe.wait_ge(edges_zeroed, img.n(2, 2))
                for j in range(3):
                    for c in range(SETS):
                        kh, kw = (2 * c + j) // 3, (2 * c + j) % 3
                        rows, first = BROWS, 0
                        if j == LAST:
                            kh, kw, rows, first = 2, 2, 1, c
                        at = BROWS * u + first + kh
                        last = nc.tensor.matmul(
                            ab_ps[(NA + u) % 3][32 * c:32 * c + 32, first * WID:(first + rows) * WID],
                            tapcols[:, j, :], f_sb[:, at:at + rows, kw:kw + WID],
                            start=(j == 0), stop=(j == LAST))
                last.then_inc(ab_summed, 1)

            def conv_c(img, i):
                u = img.c_unit(i)
                if i == 0:
                    pe.wait_ge(tapw_rest, img.n(1, 1))
                if img.is_last():
                    pe.wait_ge(fields_ready, img.n(NB, fields_needed(u)))
                elif i == 0:
                    pe.wait_ge(fields_ready, img.n(NB, NB))
                if i >= 2 and img.is_last():
                    pe.wait_ge(c_added, img.n(dve_adds(NC), i - 1))
                elif i - 2 in POOL_ADDS:
                    pe.wait_ge(c_copied, img.n(len(POOL_ADDS), POOL_ADDS.index(i - 2) + 1))
                elif i >= 2:
                    pe.wait_ge(c_added, img.n(dve_adds(NC), dve_adds(i - 1)))
                elif NC + i - 2 in POOL_ADDS:
                    wait(pe, c_copied, img.n(len(POOL_ADDS), 0))
                else:
                    wait(pe, c_added, img.n(dve_adds(NC), i - 1))
                for h in range(2):
                    a = u * CU + h * BANK
                    while a < u * CU + (h + 1) * BANK:
                        q = a // CPIX
                        b = min((q + 1) * CPIX, u * CU + (h + 1) * BANK)
                        o = a - u * CU - h * BANK
                        for part in (HEAD, REST):
                            last = nc.tensor.matmul(c_ps[(img.k + i) % 2][:, h, o:o + b - a],
                                                    tapw[img.par][part][:, q * P:(q + 1) * P],
                                                    fields[img.par][:, a - q * CPIX:b - q * CPIX],
                                                    start=(part == HEAD), stop=(part == REST))
                        a = b
                last.then_inc(c_summed, 1)

            def sum_mean(img):
                pe.wait_ge(mean_own, img.n(1, 1))
                wait(pe, gates_ready, img.n(1, 0))
                wait(pe, tapw_rest, img.n(1, 0))
                nc.tensor.matmul(mean_ps, group_avg, sm[:, 4:5], start=True, stop=True
                                 ).then_inc(mean_summed, 1)

            def sum_var(img):
                pe.wait_ge(spread_own, img.n(1, 1))
                nc.tensor.matmul(var_ps, group_avg, sm[:, 11:12], start=True, stop=True
                                 ).then_inc(var_summed, 1)

            def sum_gates(img):
                pe.wait_ge(fold_ready, img.n(1, 1))
                pe.wait_ge(maxed, img.n(THIRDS, THIRDS))
                nc.tensor.matmul(gate_ps, w1_fold[:, img.par, :], pooled[:, img.par, :], start=True,
                                 stop=True).then_inc(gates_summed, 1)

            def sum_tapw(img):
                pe.wait_ge(tapsel_ready, img.n(2, 2))
                nc.tensor.matmul(small_ps[:], tapsel[:], wf_sb[:, :, :].rearrange("p q o -> p (q o)"),
                                 start=True, stop=True).then_inc(tapw_summed, 1)

            def slot(img, s):
                done = img + -1

                def a(u):
                    if has(s, 0):
                        conv_a(img, u)

                def b(u):
                    if has(s, 0):
                        taps_b(img, u)

                def c(u):
                    if has(s, -1):
                        conv_c(done, u)

                if s == -1:
                    bias_product()
                if s == 0:
                    for u in range(NA):
                        a(u)
                    sum_tapw(img)
                    for u in range(4):
                        b(u)
                    sum_mean(img + 1)
                    b(4)
                    sum_var(img + 1)
                    b(5)
                    sum_gates(img + 1)
                    return
                if s == N - 1:
                    a(0)
                    for u in range(1, NA):
                        a(u)
                        c(u - 1)
                    c(5)
                    sum_tapw(img)
                    for u in range(NB):
                        b(u)
                        if u < 3:
                            c(6 + u)
                        elif u == 3:
                            conv_c(img, 0)
                        elif u == 4:
                            conv_c(img, 1)
                            conv_c(img, 2)
                    conv_c(img, 3)
                    return
                if s == N:
                    for i in range(EARLY, NC):
                        c(i)
                    return
                a(0)
                a(1)
                c(0)
                a(2)
                c(1)
                a(3)
                c(2)
                a(4)
                c(3)
                a(5)
                if has(s, 0):
                    sum_tapw(img)
                b(0)
                c(4)
                if s == 1:
                    b(1)
                    c(5)
                    b(2)
                    sum_mean(img + 1)
                    c(6)
                    b(3)
                    c(7)
                    b(4)
                    sum_var(img + 1)
                    c(8)
                    b(5)
                    sum_gates(img + 1)
                    return
                if has(s, 1):
                    sum_mean(img + 1)
                b(1)
                c(5)
                b(2)
                if has(s, 1):
                    sum_var(img + 1)
                c(6)
                b(3)
                c(7)
                if has(s, 1):
                    sum_gates(img + 1)
                b(4)
                c(8)
                b(5)

            run_slots(pe, slot)


def constants():
    k = np.arange(P)
    out = np.zeros((P, 2 * P + 6), np.float32)
    out[:, 0:P] = (k[:, None] // GROUP == k[None, :] // GROUP) / GROUP
    for c in range(SETS):
        for j in range(SLOTS):
            for q in range(CHUNKS):
                at = P + 32 * c + 8 * j + 2 * q
                out[q * CM:(q + 1) * CM, at:at + 2] = 1.0
    out[:, 2 * P] = -(k % 2)
    out[:, 2 * P + 1] = -0.5
    out[:, 2 * P + 2] = k < CM
    out[:, 2 * P + 3] = 1.5
    out[:, 2 * P + 4:] = 1.0 / PIX
    return out


def kernel(x, L0_conv_w1, L0_conv_b1, L0_conv_wk, L0_conv_bk, L0_conv_b_adap, L0_conv_w_fuse,
           L0_conv_b_fuse):
    import concourse.bacc as _bacc
    from concourse.bass_utils import run_bass_kernel_spmd as _run

    rep = [np.tile(np.asarray(v), CHUNKS) for v in (L0_conv_b1, L0_conv_wk, L0_conv_bk, L0_conv_b_adap)]
    arrays = {
        "x_in": np.ascontiguousarray(x).reshape(N, C, PIX),
        "w1_in": np.ascontiguousarray(np.tile(np.asarray(L0_conv_w1).T, (1, CHUNKS))),
        "vec_in": np.ascontiguousarray(np.stack([*rep, np.asarray(L0_conv_b_fuse)], axis=1)),
        "wf_in": np.ascontiguousarray(np.asarray(L0_conv_w_fuse).T),
        "const_in": constants(),
    }
    nc = _bacc.Bacc("TRN2", target_bir_lowering=False, num_devices=1)
    aps = [nc.dram_tensor(n, a.shape, mybir.dt.from_np(a.dtype), kind="ExternalInput").ap()
           for n, a in arrays.items()]
    out = nc.dram_tensor("x_out", (N, C, PIX), mybir.dt.float32, kind="ExternalOutput").ap()
    conv_kernel(nc, *aps, out)
    r = _run(nc, [arrays], core_ids=[0])
    return r.results[0]["x_out"].reshape(N, C, HGT, WID)
```
